# Optimizing a Trainium2 kernel written in Bass

```python
import numpy as np
import jax
import jax.numpy as jnp

def _softmax(x, axis=-1):
    return jax.nn.softmax(x, axis=axis)

def _gelu(x):
    return jax.nn.gelu(x, approximate=True)

def _silu(x):
    return jax.nn.silu(x)

def _sigmoid(x):
    return jax.nn.sigmoid(x)

def _layernorm(x, axis=-1, eps=1e-05):
    m = jnp.mean(x, axis=axis, keepdims=True)
    v = jnp.var(x, axis=axis, keepdims=True)
    return (x - m) / jnp.sqrt(v + eps)

def _scatter_add(tgt, idx, src, axis=0):
    return tgt.at[idx].add(src)

def _segment_sum(src, seg, n):
    return jax.ops.segment_sum(src, seg, n)
kernel_name = 'mk_decoder_postln_d1_seqx_r4_37e981'

def setup_inputs(seed: int=0):
    np.random.seed(seed)
    _w = jnp.asarray

    def _rec_inputs():
        import jax
        import jax.numpy as jnp
        _rk = jax.random.key(seed)
        x = -0.0005207 + 1.001 * jax.random.normal(jax.random.fold_in(_rk, 1), (16, 128, 256), jnp.float32)
        _lenS = 128 - jax.random.randint(jax.random.fold_in(_rk, 7), (16,), 0, max(1, 128 // 4) + 1, jnp.int32)
        _lenS2 = 128 - jax.random.randint(jax.random.fold_in(_rk, 8), (16,), 0, max(1, 128 // 4) + 1, jnp.int32)
        _ctx_512P = jax.random.normal(jax.random.fold_in(_rk, 11), (16, 16, 128), jnp.float32)
        _ctx_512c = jax.random.dirichlet(jax.random.fold_in(_rk, 511), 0.3 * jnp.ones((16,), jnp.float32), (16, 128))
        _ctx_512t = jnp.einsum('bsk,bkd->bsd', _ctx_512c, _ctx_512P)
        _ctx_512t = _ctx_512t * jax.lax.rsqrt(jnp.mean(jnp.square(_ctx_512t)) + 1e-12) * 0.953939
        ctx_512 = 0.502058 + 0.29099 * (_ctx_512t + 0.3 * jax.random.normal(jax.random.fold_in(_rk, 611), (16, 128, 128), jnp.float32))
        itok_BxS2xS_0_7 = jax.random.randint(jax.random.fold_in(_rk, 12), (16, 128, 128), 0, 8, jnp.int32)
        return (x, ctx_512, itok_BxS2xS_0_7)
    x, ctx_512, itok_BxS2xS_0_7 = _rec_inputs()

    def _L0_attn_setup():
        import jax, jax.numpy as jnp
        import numpy as np
        import math
        B, S, D, H, DH = (4, 512, 256, 8, 64)
        SCALE = 1.0 / math.sqrt(DH)
        EPS = 1e-08

        def _xavier(key, shape, gain):
            std = gain * np.sqrt(2.0 / (shape[0] + shape[1]))
            return (jax.random.normal(key, shape, jnp.float32) * std).astype(jnp.float32)

        def _stable_lse(a, b):
            m = jnp.maximum(a, b)
            return m + jnp.log1p(jnp.exp(-jnp.abs(a - b)))
        key = jax.random.key(seed)
        ks = jax.random.split(key, 7)
        return {'x': jax.random.normal(ks[0], (B, S, D), jnp.float32), 'W_q': _xavier(ks[1], (H * DH, D), 0.1), 'W_k': _xavier(ks[2], (H * DH, D), 0.1), 'W_v': _xavier(ks[3], (D, D), 1.0), 'W_alpha_w': jax.random.normal(ks[4], (H * DH, D), jnp.float32) * 0.01, 'W_alpha_b': jnp.ones((H * DH,), jnp.float32), 'W_o': _xavier(ks[5], (D, D), 0.1)}
    _L0_attn_all = _L0_attn_setup()
    _L0_attn_in = {k: v for k, v in _L0_attn_all.items() if k in ('W_q', 'W_k', 'W_v', 'W_alpha_w', 'W_alpha_b', 'W_o')}
    del _L0_attn_all

    def _L0_xattn_setup():
        import jax, jax.numpy as jnp
        import numpy as np
        key = jax.random.key(seed)
        k1, k2, k3, k4, k5 = jax.random.split(key, 5)
        B, K, S, E, I, D = (4, 2, 128, 8, 256, 512)
        x = jax.random.normal(k1, (B, S, I), dtype=jnp.float32)
        weights = jax.random.uniform(k2, (B, K, S), dtype=jnp.float32)
        ensembles = jax.random.randint(k3, (B, K, S), 0, E, dtype=jnp.int64)
        lim1 = float(np.sqrt(6.0 / (D + I)))
        proj_in = jax.random.uniform(k4, (E, D, I), dtype=jnp.float32, minval=-lim1, maxval=lim1)
        proj_out = jax.random.uniform(k5, (E, I, D), dtype=jnp.float32, minval=-lim1, maxval=lim1)
        return {'x': x, 'weights': weights, 'ensembles': ensembles, 'proj_in': proj_in, 'proj_out': proj_out}
    _L0_xattn_all = _L0_xattn_setup()
    _L0_xattn_in = {k: v for k, v in _L0_xattn_all.items() if k in ('proj_in', 'proj_out')}
    del _L0_xattn_all

    def _L0_ffn_setup():
        import jax, jax.numpy as jnp
        import numpy as np
        D_IN, D_HID = (256, 1024)

        def _ternary(key, shape):
            return jax.random.randint(key, shape, -1, 2).astype(jnp.float32)

        def _tlin(x, w, s):
            return jnp.einsum('bsi,oi->bso', x, w) * s
        key = jax.random.key(seed)
        ks = jax.random.split(key, 12)
        inv = lambda fan: 1.0 / np.sqrt(fan).astype(np.float32)
        return {'x': jax.random.normal(ks[0], (4, 512, D_IN), dtype=jnp.float32), 'w1_w': _ternary(ks[1], (D_HID, D_IN)), 'w1_s': jax.random.uniform(ks[2], (D_HID,), dtype=jnp.float32) * inv(D_IN), 'w2_w': _ternary(ks[3], (D_HID, D_IN)), 'w2_s': jax.random.uniform(ks[4], (D_HID,), dtype=jnp.float32) * inv(D_IN), 'h1_w': _ternary(ks[5], (D_HID, D_HID)), 'h1_s': jax.random.uniform(ks[6], (D_HID,), dtype=jnp.float32) * inv(D_HID), 'h2_w': _ternary(ks[7], (D_HID, D_HID)), 'h2_s': jax.random.uniform(ks[8], (D_HID,), dtype=jnp.float32) * inv(D_HID), 'w3_w': _ternary(ks[9], (D_IN, D_HID)), 'w3_s': jax.random.uniform(ks[10], (D_IN,), dtype=jnp.float32) * inv(D_HID)}
    _L0_ffn_all = _L0_ffn_setup()
    _L0_ffn_in = {k: v for k, v in _L0_ffn_all.items() if k in ('w1_w', 'w1_s', 'w2_w', 'w2_s', 'h1_w', 'h1_s', 'h2_w', 'h2_s', 'w3_w', 'w3_s')}
    del _L0_ffn_all
    return {'x': x, 'ctx_512': ctx_512, 'itok_BxS2xS_0_7': itok_BxS2xS_0_7, 'L0_attn_W_q': _L0_attn_in['W_q'], 'L0_attn_W_k': _L0_attn_in['W_k'], 'L0_attn_W_v': _L0_attn_in['W_v'], 'L0_attn_W_alpha_w': _L0_attn_in['W_alpha_w'], 'L0_attn_W_alpha_b': _L0_attn_in['W_alpha_b'], 'L0_attn_W_o': _L0_attn_in['W_o'], 'L0_xattn_proj_in': _L0_xattn_in['proj_in'], 'L0_xattn_proj_out': _L0_xattn_in['proj_out'], 'L0_ffn_w1_w': _L0_ffn_in['w1_w'], 'L0_ffn_w1_s': _L0_ffn_in['w1_s'], 'L0_ffn_w2_w': _L0_ffn_in['w2_w'], 'L0_ffn_w2_s': _L0_ffn_in['w2_s'], 'L0_ffn_h1_w': _L0_ffn_in['h1_w'], 'L0_ffn_h1_s': _L0_ffn_in['h1_s'], 'L0_ffn_h2_w': _L0_ffn_in['h2_w'], 'L0_ffn_h2_s': _L0_ffn_in['h2_s'], 'L0_ffn_w3_w': _L0_ffn_in['w3_w'], 'L0_ffn_w3_s': _L0_ffn_in['w3_s']}

def reference(x, ctx_512, itok_BxS2xS_0_7, L0_attn_W_q, L0_attn_W_k, L0_attn_W_v, L0_attn_W_alpha_w, L0_attn_W_alpha_b, L0_attn_W_o, L0_xattn_proj_in, L0_xattn_proj_out, L0_ffn_w1_w, L0_ffn_w1_s, L0_ffn_w2_w, L0_ffn_w2_s, L0_ffn_h1_w, L0_ffn_h1_s, L0_ffn_h2_w, L0_ffn_h2_s, L0_ffn_w3_w, L0_ffn_w3_s):
    import jax
    import jax.numpy as jnp

    def _L0_attn_ref(x, W_q, W_k, W_v, W_alpha_w, W_alpha_b, W_o):
        import jax, jax.numpy as jnp
        import numpy as np
        import math
        B, S, D, H, DH = (4, 512, 256, 8, 64)
        SCALE = 1.0 / math.sqrt(DH)
        EPS = 1e-08

        def _xavier(key, shape, gain):
            std = gain * np.sqrt(2.0 / (shape[0] + shape[1]))
            return (jax.random.normal(key, shape, jnp.float32) * std).astype(jnp.float32)

        def _stable_lse(a, b):
            m = jnp.maximum(a, b)
            return m + jnp.log1p(jnp.exp(-jnp.abs(a - b)))
        Bx, Sx, _ = x.shape
        q = (x @ W_q.T).reshape(Bx, Sx, H, DH)
        k = (x @ W_k.T).reshape(Bx, Sx, H, DH)
        v = x @ W_v.T
        b = (q * k).sum(-1) * SCALE
        alpha = (x @ W_alpha_w.T + W_alpha_b).reshape(Bx, Sx, H, DH)
        a = -jax.nn.softplus(alpha).sum(-1)
        vs = jnp.sign(v)
        vs = jnp.where(vs == 0, jnp.ones_like(vs), vs)
        vl = jnp.log(jnp.abs(v) + EPS)
        ln0 = b[:, 0]
        nm0 = b[:, 0, :, None] + vl[:, 0, None, :]
        sg0 = jnp.broadcast_to(vs[:, 0, None, :], nm0.shape)
        y0 = (sg0 * jnp.exp(nm0 - ln0[..., None])).sum(-2)

        def step(carry, inp):
            ln, nm, sg = carry
            a_t, b_t, vl_t, vs_t = inp
            ln = _stable_lse(a_t + ln, b_t)
            dec = a_t[..., None] + nm
            new = b_t[..., None] + vl_t[:, None, :]
            m = jnp.maximum(dec, new)
            ssum = sg * jnp.exp(dec - m) + vs_t[:, None, :] * jnp.exp(new - m)
            nsg = jnp.sign(ssum)
            nsg = jnp.where(nsg == 0, jnp.ones_like(nsg), nsg)
            nm = m + jnp.log(jnp.abs(ssum) + EPS)
            y = (nsg * jnp.exp(nm - ln[..., None])).sum(-2)
            return ((ln, nm, nsg), y)
        xs = (jnp.moveaxis(a[:, 1:], 1, 0), jnp.moveaxis(b[:, 1:], 1, 0), jnp.moveaxis(vl[:, 1:], 1, 0), jnp.moveaxis(vs[:, 1:], 1, 0))
        _, ys = jax.lax.scan(step, (ln0, nm0, sg0), xs)
        y = jnp.concatenate([y0[:, None, :], jnp.moveaxis(ys, 0, 1)], axis=1)
        return y @ W_o.T

    def _L0_xattn_ref(x, weights, ensembles, proj_in, proj_out):
        import jax, jax.numpy as jnp
        import numpy as np
        E = proj_in.shape[0]
        h = jax.nn.relu(jnp.einsum('edi,bsi->bsed', proj_in, x))
        o = jnp.einsum('eid,bsed->bsei', proj_out, h)
        onehot = jax.nn.one_hot(ensembles, E, dtype=x.dtype)
        gate = jnp.einsum('bks,bkse->bse', weights, onehot)
        return jnp.einsum('bsei,bse->bsi', o, gate)

    def _L0_ffn_ref(x, w1_w, w1_s, w2_w, w2_s, h1_w, h1_s, h2_w, h2_s, w3_w, w3_s):
        import jax, jax.numpy as jnp
        import numpy as np
        D_IN, D_HID = (256, 1024)

        def _ternary(key, shape):
            return jax.random.randint(key, shape, -1, 2).astype(jnp.float32)

        def _tlin(x, w, s):
            return jnp.einsum('bsi,oi->bso', x, w) * s
        h = jax.nn.silu(_tlin(x, w1_w, w1_s)) * _tlin(x, w2_w, w2_s)
        h = jax.nn.gelu(_tlin(h, h1_w, h1_s), approximate=False)
        h = jax.nn.gelu(_tlin(h, h2_w, h2_s), approximate=False)
        return _tlin(h, w3_w, w3_s)
    x = _layernorm(x + _L0_attn_ref(x, L0_attn_W_q, L0_attn_W_k, L0_attn_W_v, L0_attn_W_alpha_w, L0_attn_W_alpha_b, L0_attn_W_o), axis=-1)
    x = _layernorm(x + _L0_xattn_ref(x, ctx_512, itok_BxS2xS_0_7, L0_xattn_proj_in, L0_xattn_proj_out), axis=-1)
    x = _layernorm(x + _L0_ffn_ref(x, L0_ffn_w1_w, L0_ffn_w1_s, L0_ffn_w2_w, L0_ffn_w2_s, L0_ffn_h1_w, L0_ffn_h1_s, L0_ffn_h2_w, L0_ffn_h2_s, L0_ffn_w3_w, L0_ffn_w3_s), axis=-1)
    return x

_drawn_inputs = setup_inputs


def setup_inputs(seed=0):
    import zlib

    import numpy as np

    out = dict(_drawn_inputs(seed))
    spreads = {'L0_attn_W_alpha_b': (1.0, 0.2)}
    factors = {'L0_attn_W_q': 8.0,
     'L0_attn_W_k': 8.0,
     'L0_ffn_w1_w': 8.0,
     'L0_ffn_w1_s': 8.0,
     'L0_ffn_w2_w': 8.0,
     'L0_ffn_w2_s': 8.0,
     'L0_ffn_h1_w': 8.0,
     'L0_ffn_h1_s': 8.0,
     'L0_ffn_h2_w': 8.0,
     'L0_ffn_h2_s': 8.0,
     'L0_ffn_w3_w': 8.0,
     'L0_ffn_w3_s': 8.0}
    for name, (base, spread) in spreads.items():
        noise = np.random.default_rng([zlib.crc32(name.encode()), seed]).standard_normal(out[name].shape)
        drawn = base * np.exp(spread * noise) if base else spread * noise
        out[name] = jnp.asarray(drawn.astype(out[name].dtype))
    for name, factor in factors.items():
        out[name] = (out[name] * factor).astype(out[name].dtype)
    return out
```

```python
import math
from contextlib import ExitStack

import numpy as np

import concourse.bass as bass
from concourse import mybir

F32 = mybir.dt.float32
F32R = mybir.dt.float32r
I32 = mybir.dt.int32
ALU = mybir.AluOpType
ACT = mybir.ActivationFunctionType
AX_X = mybir.AxisListType.X
RMAX = bass.bass_isa.ReduceOp.max

P = 128
B, S, D = 16, 128, 256
H, DH = 8, 64
HD = H * DH
E, DX = 8, 512
F = 1024
DC, XC, FC = D // P, DX // P, F // P
J = 4
G = B // J
N = J * S
WP = 3 * HD + D
WX = DC * DX + XC * D
WF = 2 * DC * F + 2 * FC * F + FC * D
CH = WF // 32
LN_EPS = 1e-5
EPS = 1e-8
SCALE = 1.0 / math.sqrt(DH)
LOWEST = -3.0e38
assert S == P and B * H == P and WF % 32 == 0


def decoder_kernel(nc, x, xT, wproj, wo, alpha_b, ctx, itok, wx, wffn, ffn_s, w3_s, out):
    with ExitStack() as stack:
        base = [16512]

        def region(nbytes):
            at = base[0]
            base[0] += nbytes
            return at

        def at(name, offset, shape, dt=F32):
            return nc.alloc_sbuf_tensor_at(name, [P, *shape], dt, offset=offset)

        def at_r(name, offset, shape):
            return at(name, offset, shape, F32R)

        def both(name, offset, shape):
            return at(name + "_r", offset, shape, F32R), at(name + "_f", offset, shape)

        def sem(name):
            return stack.enter_context(nc.semaphore(name))

        o_x, o_xh, o_xl = region(B * D * 4), region(B * D * 4), region(B * D * 4)
        o_w, o_ha, o_hb = region(WF * 4), region(2 * FC * N * 4), region(2 * FC * N * 4)

        x_tok = at("x_tok", o_x, [B, D])
        xT_hi = at_r("xT_hi", o_xh, [DC, B * S])
        xT_lo = at_r("xT_lo", o_xl, [DC, B * S])
        def small(name, shape, dt=F32):
            return at(name, region(-(-4 * math.prod(shape) // 32) * 32), shape, dt)

        gates, ident, scales, neq = small("gates", [B, E]), small("ident", [P]), small("scales", [4, FC]), small("neq", [32])
        expert_no = small("expert_no", [E])
        bn, mv, var_eps = small("bn", [J, 6]), small("mv", [J, 2]), small("var_eps", [J])
        rstd, neghalf = small("rstd", [J]), small("neghalf", [J])
        vstat, vall, cond, cond_all = small("vstat", [2]), small("vall", [2]), small("cond", [1]), small("cond_all", [1])
        wide_col, wide_all = small("wide_col", [1]), small("wide_all", [1])
        flag, wide_flag = small("flag", [1], I32), small("wide_flag", [1], I32)
        stage = small("stage", [2, CH])
        assert base[0] <= 229344

        x0T = at("x0T", o_xl, [B, DC, S])
        wp_hi = at_r("wp_hi", o_w, [DC, WP])
        wp_lo, wp_raw = both("wp_lo", o_w + 14336, [DC, WP])
        wo_hi = at_r("wo_hi", o_w + 28672, [DC, D])
        wo_lo, wo_raw = both("wo_lo", o_w + 30720, [DC, D])
        v_sb = at("v_sb", o_w + 32768, [B, D])
        bias_b = at("bias_b", o_w + 49152, [HD])
        q_sb = at("q_sb", o_w + 51200, [2, HD])
        k_sb = at("k_sb", o_w + 55296, [2, HD])
        qk = at("qk", o_w + 59392, [2, HD])
        al = at("al", o_w + 63488, [2, HD])
        sp = at("sp", o_w + 67584, [2, HD])
        ctx_sb = at("ctx_sb", o_w + 71680, [B, S])
        itok_sb = at("itok_sb", o_w + 79872, [B, S], I32)
        mask = at("mask", o_ha, [2, B, S])
        xs_hi = at_r("xs_hi", o_ha + 16384, [J, DC, S])
        xs_lo = at_r("xs_lo", o_ha + 20480, [J, DC, S])
        b_tok = at("b_tok", o_ha + 24576, [B, H])
        a_tok = at("a_tok", o_ha + 25088, [B, H])
        sgn = at("sgn", o_ha + 25600, [D])
        ident8 = at("ident8", o_ha + 28672, [H * S])
        bT, aT, mT, decT, betT, eT, rT, BT, AT, B_tok, val = (
            at(n, o_w + 65536 + 512 * i, [S]) for i, n in enumerate(
                ["bT", "aT", "mT", "decT", "betT", "eT", "rT", "BT", "AT", "B_tok", "val"]))
        M_f = at("M_f", o_w + 51200, [J, S])
        M_hi = at_r("M_hi", o_w + 53248, [J, S])
        M_lo = at_r("M_lo", o_w + 55296, [J, S])
        vs_hi = at_r("vs_hi", o_w + 57344, [J, D])
        vs_lo = at_r("vs_lo", o_w + 61440, [J, D])
        decay = at("decay", o_w + 71680, [J, H * S])
        junk = at("junk", o_w + 71680, [B * D])
        a_bc = at("a_bc", o_ha, [J, H * S])
        yT_hi = at_r("yT_hi", o_ha + 16384, [J, DC, S])
        yT_lo = at_r("yT_lo", o_ha + 20480, [J, DC, S])
        xn = at("xn", o_ha + 24576, [J, D])
        r_now, v_now, n_now, raw_now, mx_now, sg_now = (
            at(n, o_w + 71680 + 1024 * i, [D]) for i, n in enumerate(
                ["r_now", "v_now", "n_now", "raw_now", "mx_now", "sg_now"]))
        r_heads = at("r_heads", o_w + 79872, [H, D])
        wx_hi = at_r("wx_hi", o_hb, [2, WX])
        wx_lo, wx_raw = both("wx_lo", o_hb + 2 * WX * 4, [2, WX])
        hx_hi = at_r("hx_hi", o_ha, [2, XC, N])
        hx_lo = at_r("hx_lo", o_ha + 2 * XC * N * 4, [2, XC, N])
        wf_hi, wf_raw = both("wf_hi", o_w, [WF])
        xf_hi, xf_wide = both("xf_hi", o_xh, [DC, N])
        xf_lo = at_r("xf_lo", o_xh + 4096, [DC, N])
        s3_b = at("s3_b", o_xh + 8192, [D])
        y_s = at("y_s", o_xh + 9216, [2, D])
        xo = at("xo", o_xh + 12288, [J, D])
        silu = at("silu", o_xl, [2, N])
        hf = at("hf", o_xl + 4096, [3, N])
        xn2 = at("xn2", o_xl + 10240, [J, D])
        ha_hi, ha_wide = both("ha_hi", o_ha, [FC, N])
        ha_lo = at_r("ha_lo", o_ha + FC * N * 4, [FC, N])
        hb_hi, hb_wide = both("hb_hi", o_hb, [FC, N])
        hb_lo = at_r("hb_lo", o_hb + FC * N * 4, [FC, N])

        bank = [stack.enter_context(nc.psum_tensor(f"bank{i}", [P, 512], F32)) for i in range(8)]

        a_dram = nc.dram_tensor("a_dram", (P, S), F32, kind="Internal").ap()
        v_dram = nc.dram_tensor("v_dram", (B, S, D), F32, kind="Internal").ap()
        r_dram = nc.dram_tensor("r_dram", (P, S, D), F32, kind="Internal").ap()

        s_x0T_first = sem("x0T_first")
        s_x0T_in = sem("x0T_in")
        s_xtok_in = sem("xtok_in")
        s_bias_in = sem("bias_in")
        s_wo_in = sem("wo_in")
        s_gate_in = sem("gate_in")
        s_small_in = sem("small_in")
        s_s3_in = sem("s3_in")
        s_const_ok = sem("const_ok")
        s_wp_hi_ok = sem("wp_hi_ok")
        s_wp_lo_ok = sem("wp_lo_ok")
        s_wo_hi_ok = sem("wo_hi_ok")
        s_wo_lo_ok = sem("wo_lo_ok")
        s_xs_hi_ok = sem("xs_hi_ok")
        s_xs_lo_ok = sem("xs_lo_ok")
        s_q_mm = sem("q_mm")
        s_k_mm = sem("k_mm")
        s_a_mm = sem("a_mm")
        s_v_mm = sem("v_mm")
        s_q_out = sem("q_out")
        s_k_out = sem("k_out")
        s_al_out = sem("al_out")
        s_v_out = sem("v_out")
        s_abs_ok = sem("abs_ok")
        s_exp_ok = sem("exp_ok")
        s_ln_ok = sem("ln_ok")
        s_qk_ok = sem("qk_ok")
        s_sgn_ok = sem("sgn_ok")
        s_sp_sum = sem("sp_sum")
        s_sp_ok = sem("sp_ok")
        s_b_red = sem("b_red")
        s_mask_ok = sem("mask_ok")
        s_gate_mm = sem("gate_mm")
        s_gates_ok = sem("gates_ok")
        s_ba_T = sem("ba_T")
        s_chain = sem("chain")
        s_tab_d = sem("tab_d")
        s_tab_exp = sem("tab_exp")
        s_A_ok = sem("A_ok")
        s_B_T = sem("B_T")
        s_BtokOK = sem("BtokOK")
        s_A_out = sem("A_out")
        s_vstat_ok = sem("vstat_ok")
        s_vall_ok = sem("vall_ok")
        s_cond_ok = sem("cond_ok")
        s_condall_ok = sem("condall_ok")
        s_flag_ok = sem("flag_ok")
        s_attn_ready = sem("attn_ready")
        s_fall_v = sem("fall_v")
        s_fall_vin = sem("fall_vin")
        s_fall_step = sem("fall_step")
        s_fall_chain = sem("fall_chain")
        s_fall_r = sem("fall_r")
        s_fall_rin = sem("fall_rin")
        s_fall_sum = sem("fall_sum")
        s_scan_ok = sem("scan_ok")
        s_wB_ok = sem("wB_ok")
        s_M_ok = sem("M_ok")
        s_Mhi_ok = sem("Mhi_ok")
        s_vhi_ok = sem("vhi_ok")
        s_Mlo_ok = sem("Mlo_ok")
        s_vlo_ok = sem("vlo_ok")
        s_y_mm = sem("y_mm")
        s_yhi_ok = sem("yhi_ok")
        s_ylo_ok = sem("ylo_ok")
        s_o_mm = sem("o_mm")
        s_res_ok = sem("res_ok")
        s_bn_tick = sem("bn_tick")
        s_bn_ok = sem("bn_ok")
        s_mv_ok = sem("mv_ok")
        s_ve_ok = sem("ve_ok")
        s_rstd_ok = sem("rstd_ok")
        s_xn_ok = sem("xn_ok")
        s_xkeep_ok = sem("xkeep_ok")
        s_xT_mm = sem("xT_mm")
        s_xThi_ok = sem("xThi_ok")
        s_xTlo_ok = sem("xTlo_ok")
        s_up_mm = sem("up_mm")
        s_relu_ok = sem("relu_ok")
        s_hlo_ok = sem("hlo_ok")
        s_down_mm = sem("down_mm")
        s_gated_ok = sem("gated_ok")
        s_wxhi_ok = sem("wxhi_ok")
        s_wxlo_ok = sem("wxlo_ok")
        s_stage_used = sem("stage_used")
        s_st_cmp = sem("st_cmp")
        s_wide_c = sem("wide_c")
        s_wide_a = sem("wide_a")
        s_wide_f = sem("wide_f")
        s_raw_in = sem("raw_in")
        s_f_bn = sem("f_bn")
        s_f_mv = sem("f_mv")
        s_f_ve = sem("f_ve")
        s_f_rstd = sem("f_rstd")
        s_f_xn = sem("f_xn")
        s_f_keep = sem("f_keep")
        s_f_T = sem("f_T")
        s_f_xhi = sem("f_xhi")
        s_f_xlo = sem("f_xlo")
        s_f_mm = sem("f_mm")
        s_l_out = sem("l_out")
        s_f_silu = sem("f_silu")
        s_f_hf = sem("f_hf")
        s_f_hi = sem("f_hi")
        s_f_lo = sem("f_lo")
        s_e_y = sem("e_y")
        s_e_mul = sem("e_mul")
        s_e_add = sem("e_add")
        s_e_bn = sem("e_bn")
        s_e_mv = sem("e_mv")
        s_e_ve = sem("e_ve")
        s_e_rstd = sem("e_rstd")
        s_e_xo = sem("e_xo")
        wp_in = [sem(f"wp_in{n}") for n in range(4)]
        abc_in = [sem(f"abc_in{j}") for j in range(J)]
        stage_in = [sem(f"stage_in{u}") for u in range(2)]
        wx_in = [sem(f"wx_in{e}") for e in range(2)]
        out_done = [sem(f"out_done{j}") for j in range(J)]

        block = stack.enter_context(nc.Block())

        def groups(eng, body, *more):
            with eng.Fori(0, G - 1) as g:
                body(g, False, *more)
            body(G - 1, True, *more)

        COLS = {"q": (0, HD), "k": (HD, HD), "a": (2 * HD, HD), "v": (3 * HD, D)}

        def step_path_dma(sp_):
            sp_.dma_start(v_dram.rearrange("b t d -> t b d"), v_sb[:, :, :]).then_inc(s_fall_v, 16)
            sp_.wait_ge(s_fall_v, 16)
            with sp_.Fori(0, S) as t:
                sp_.wait_ge(s_fall_step, t + 1)
                sp_.dma_start(v_now[:, :], v_dram[:, bass.ds(t, 1), :].rearrange("b o d -> b (o d)").unsqueeze(1).to_broadcast([B, H, D])
                              ).then_inc(s_fall_vin, 16)
                sp_.wait_ge(s_fall_r, t + 1)
                sp_.dma_start(r_dram[:, bass.ds(t, 1), :].rearrange("p o d -> p (o d)"), r_now[:, :]).then_inc(s_fall_rin, 16)
            sp_.wait_ge(s_fall_rin, 16 * S + 16)
            with sp_.Fori(0, B) as b:
                sp_.wait_ge(s_fall_sum, b + 1)
                sp_.dma_start(r_heads[:, :, :], r_dram[bass.ds(b * H, H)].rearrange("h t d -> t h d")).then_inc(s_fall_rin, 16)
            sp_.wait_ge(s_fall_sum, B + 1)
            sp_.dma_start(a_dram, AT[:, :]).then_inc(s_A_out, 16)
            sp_.wait_ge(s_A_out, 32)

        def step_path(dve):
            dve.sem_inc(s_fall_step, 1)
            dve.sem_inc(s_fall_rin, 16)
            dve.sem_inc(s_fall_sum, 1)
            dve.memset(r_now[:, :], 0.0)
            with dve.Fori(0, S) as t:
                a_t, b_t = AT[:, bass.ds(t, 1)], BT[:, bass.ds(t, 1)]
                dve.wait_ge(s_fall_vin, t * 16 + 16)
                dve.tensor_scalar(n_now[:, :], v_now[:, :], b_t, None, ALU.mult).then_inc(s_fall_step, 1)
                dve.wait_ge(s_fall_step, t + 2)
                dve.scalar_tensor_tensor(out=raw_now[:, :], in0=r_now[:, :], scalar=a_t, in1=n_now[:, :],
                                         op0=ALU.mult, op1=ALU.add)
                dve.scalar_tensor_tensor(out=mx_now[:, :], in0=r_now[:, :], scalar=a_t, in1=n_now[:, :],
                                         op0=ALU.mult, op1=ALU.max)
                dve.scalar_tensor_tensor(out=sg_now[:, :], in0=r_now[:, :], scalar=a_t, in1=n_now[:, :],
                                         op0=ALU.mult, op1=ALU.min).then_inc(s_fall_chain, 1)
                dve.wait_ge(s_fall_chain, t * 4 + 1)
                dve.scalar_tensor_tensor(out=mx_now[:, :], in0=sg_now[:, :], scalar=-1.0, in1=mx_now[:, :],
                                         op0=ALU.mult, op1=ALU.max).then_inc(s_fall_chain, 1)
                dve.wait_ge(s_fall_chain, t * 4 + 2)
                dve.tensor_scalar(sg_now[:, :], raw_now[:, :], 0.0, 2.0, ALU.is_ge, ALU.mult).then_inc(s_fall_chain, 1)
                dve.wait_ge(s_fall_chain, t * 4 + 3)
                dve.scalar_tensor_tensor(out=sg_now[:, :], in0=sg_now[:, :], scalar=1.0, in1=mx_now[:, :],
                                         op0=ALU.subtract, op1=ALU.mult).then_inc(s_fall_chain, 1)
                dve.wait_ge(s_fall_chain, t * 4 + 4)
                dve.wait_ge(s_fall_rin, t * 16 + 16)
                dve.scalar_tensor_tensor(out=r_now[:, :], in0=sg_now[:, :], scalar=EPS, in1=raw_now[:, :],
                                         op0=ALU.mult, op1=ALU.add).then_inc(s_fall_r, 1)
                dve.wait_ge(s_fall_r, t + 1)
            dve.memset(AT[:, :], 0.0)
            dve.memset(B_tok[:, :], 1.0 / H)
            with dve.Fori(0, B) as b:
                dve.wait_ge(s_fall_rin, 16 * S + 16 + 16 + b * 16)
                dve.tensor_reduce(v_sb[:, bass.ds(b, 1)].rearrange("p o d -> p (o d)"), r_heads[:, :, :].rearrange("p h d -> p d h"),
                                  AX_X, ALU.add).then_inc(s_fall_sum, 1)

        @block.sync
        def _(sp_):
            for i, name in enumerate("qkav"):
                c0, n = COLS[name]
                sp_.dma_start(wp_raw[:, :, c0:c0 + n], wproj[:, :, c0:c0 + n]).then_inc(wp_in[i], 16)
                if i == 0:
                    sp_.dma_start(x0T[:, 0:J], xT[:, 0:J]).then_inc(s_x0T_first, 16)
            sp_.dma_start(bias_b[:, :], alpha_b.partition_broadcast(P)).then_inc(s_bias_in, 16)
            for g in range(1, G):
                sp_.dma_start(x0T[:, J * g:J * g + J], xT[:, J * g:J * g + J]).then_inc(s_x0T_in, 16)
            sp_.dma_start(ctx_sb[:, :, :], ctx.rearrange("b k s -> k b s")).then_inc(s_gate_in, 16)
            sp_.dma_start(itok_sb[:, :, :], itok.rearrange("b k s -> k b s")).then_inc(s_gate_in, 16)
            sp_.dma_start(wo_raw[:, :, :], wo).then_inc(s_wo_in, 16)
            sp_.dma_start(x_tok[:, :, :], x.rearrange("b t d -> t b d")).then_inc(s_xtok_in, 16)
            sp_.dma_start(scales[:, :, :], ffn_s).then_inc(s_small_in, 16)
            sp_.dma_start(wx_raw[:, 0], wx[0]).then_inc(wx_in[0], 16)

            sp_.wait_ge(s_A_ok, 1)
            sp_.dma_start(a_dram, AT[:, :]).then_inc(s_A_out, 16)
            sp_.wait_ge(s_flag_ok, 1)
            stepwise = sp_.value_load(flag[0:1, 0:1], min_val=0, max_val=1)
            sp_.wait_ge(s_A_out, 16)
            with sp_.If(stepwise > 0):
                step_path_dma(sp_)
            with sp_.Else():
                sp_.nop()
            sp_.wait_ge(s_attn_ready, 1)

            def decays(g):
                for j in range(J):
                    sp_.wait_ge(s_scan_ok, g * J + j + 1)
                    sp_.dma_start(a_bc[:, j], a_dram[bass.ds((g * J + j) * H, H), :].rearrange("h s -> (h s)").partition_broadcast(P)
                                  ).then_inc(abc_in[j], 16)
            with sp_.Fori(0, G) as g:
                decays(g)

            sp_.wait_ge(s_xTlo_ok, B + J)
            with sp_.Fori(0, E // 2) as p:
                for u in range(8):
                    sp_.wait_ge(s_stage_used, p * 8 + u + 1)
                    sp_.dma_start(stage[:, u % 2], wffn[:, bass.ds((p * 8 + u) * CH, CH)]).then_inc(stage_in[u % 2], 16)
                    if u == 1:
                        sp_.wait_ge(s_down_mm, p * 8 * J + 2 * J)
                        sp_.dma_start(wx_raw[:, 1], wx[bass.ds(p * 2 + 1, 1)].rearrange("e p w -> p (e w)")).then_inc(wx_in[1], 16)
                    if u == 4:
                        sp_.wait_ge(s_down_mm, (p * 8 + 4) * J + 2 * J)
                        sp_.dma_start(wx_raw[:, 0], wx[bass.ds((p * 2 + 2) % E, 1)].rearrange("e p w -> p (e w)")).then_inc(wx_in[0], 16)
            sp_.wait_ge(s_gated_ok, B * E + J)
            sp_.dma_start(s3_b[:, :], w3_s.partition_broadcast(P)).then_inc(s_s3_in, 16)
            sp_.wait_ge(s_wide_f, 1)
            wide = sp_.value_load(wide_flag[0:1, 0:1], min_val=0, max_val=1)

            with sp_.If(wide > 0):
                sp_.dma_start(wf_raw[:, :], wffn).then_inc(s_raw_in, 16)
            with sp_.Else():
                sp_.nop()

            with sp_.Fori(0, G) as g:
                for j in range(J):
                    sp_.wait_ge(s_e_xo, g * J + j + 1)
                    sp_.dma_start(out[bass.ds(g * J + j, 1)].rearrange("b t d -> t (b d)"), xo[:, j]).then_inc(out_done[j], 16)
            for j in range(J):
                sp_.wait_ge(out_done[j], 16 * G + 16)

        @block.gpsimd
        def _(pool):
            pool.memset(ident[:, :], 0.0).then_inc(s_const_ok, 1)
            pool.memset(neghalf[:, :], -0.5)
            for e in range(E):
                pool.memset(expert_no[:, e:e + 1], float(e))
            pool.wait_ge(s_const_ok, 1)
            pool.affine_select(out=ident[:, :], in_=ident[:, :], compare_op=ALU.not_equal, fill=1.0, base=0,
                               pattern=[[-1, P]], channel_multiplier=1).then_inc(s_const_ok, 1)
            pool.wait_ge(s_const_ok, 2)
            for h in range(H):
                c = pool.tensor_copy(ident8[:, h * S:h * S + S], ident[:, :])
            c.then_inc(s_const_ok, 1)

            def low_half(t, j):
                pool.wait_ge(s_xs_hi_ok, t + 1)
                pool.tensor_tensor(xs_lo[:, j], x0T[:, bass.ds(t, 1)].rearrange("p o c s -> p (o c) s"), xs_hi[:, j].bitcast(F32),
                                   ALU.subtract).then_inc(s_xs_lo_ok, 1)

            for j in range(J):
                low_half(j, j)

            def project(g, last):
                for j in range(J):
                    t = g * J + j
                    pool.wait_ge(s_k_out, t + 3)
                    pool.wait_ge(s_b_red, t + 1)
                    pool.tensor_tensor(qk[:, j % 2], q_sb[:, j % 2], k_sb[:, j % 2], ALU.mult).then_inc(s_qk_ok, 1)
                    if not last:
                        pool.wait_ge(s_v_mm, t + 1)
                        low_half(t + J, j)
            groups(pool, project)

            pool.wait_ge(s_vstat_ok, 2)
            pool.partition_all_reduce(vall[:, :], vstat[:, :], P, RMAX).then_inc(s_vall_ok, 1)
            pool.wait_ge(s_cond_ok, 1)
            pool.partition_all_reduce(cond_all[:, :], cond[:, :], P, RMAX).then_inc(s_condall_ok, 1)

            def mix(g, last):
                for j in range(J):
                    t = g * J + j
                    if j == 0:
                        pool.wait_ge(s_vhi_ok, g * J + J)
                    pool.wait_ge(s_y_mm, t + 1)
                    pool.tensor_tensor(vs_lo[:, j], v_sb[:, bass.ds(t, 1)].rearrange("p o d -> p (o d)"), vs_hi[:, j].bitcast(F32),
                                       ALU.subtract).then_inc(s_vlo_ok, 1)
                for j in range(J):
                    t = g * J + j
                    pool.wait_ge(s_scan_ok, t + 1 + J)
                    dec = decay[:, j].rearrange("p (h s) -> p h s", h=H)
                    pool.tensor_tensor(dec, dec, B_tok[:, bass.ds(t * H, H)].unsqueeze(2).to_broadcast([P, H, S]),
                                       ALU.mult).then_inc(s_wB_ok, 1)
                for j in range(J):
                    t = g * J + j
                    pool.wait_ge(s_Mhi_ok, t + 1)
                    pool.tensor_tensor(M_lo[:, j], M_f[:, j], M_hi[:, j].bitcast(F32), ALU.subtract).then_inc(s_Mlo_ok, 1)
                pool.wait_ge(s_ve_ok, g + 1)
                pool.tensor_tensor(rstd[:, :], var_eps[:, :], neghalf[:, :], ALU.pow).then_inc(s_rstd_ok, 1)
            pool.wait_ge(s_attn_ready, 1)
            with pool.Fori(0, G) as g:
                mix(g, False)

            def expert_low(e, n):
                pool.wait_ge(s_wxhi_ok, n * 4 + 4)
                for c in range(4):
                    a = slice(c * WX // 4, (c + 1) * WX // 4)
                    pool.tensor_tensor(wx_lo[:, e, a], wx_raw[:, e, a], wx_hi[:, e, a].bitcast(F32), ALU.subtract).then_inc(s_wxlo_ok, 1)
            expert_low(0, 0)
            with pool.Fori(0, E // 2) as p:
                expert_low(1, p * 2 + 1)
                expert_low(0, p * 2 + 2)
            pool.wait_ge(s_wide_c, 1)
            pool.partition_all_reduce(wide_all[:, :], wide_col[:, :], P, RMAX).then_inc(s_wide_a, 1)

            def ln_rstd(sem_in, sem_out, n):
                pool.wait_ge(sem_in, n)
                pool.tensor_tensor(rstd[:, :], var_eps[:, :], neghalf[:, :], ALU.pow).then_inc(sem_out, 1)
            ln_rstd(s_f_ve, s_f_rstd, 1)
            pool.wait_ge(s_wide_f, 1)
            wide = pool.value_load(wide_flag[0:1, 0:1], min_val=0, max_val=1)

            def ffn(g, last, exact):
                if exact:
                    for n in range(3 * FC):
                        pool.wait_ge(s_f_hi, g * 3 * FC + n + 1)
                        dst, hi = [(ha_lo, ha_hi), (hb_lo, hb_hi), (ha_lo, ha_hi)][n // FC]
                        pool.tensor_tensor(dst[:, n % FC], hf[:, n % 3], hi[:, n % FC].bitcast(F32), ALU.subtract).then_inc(s_f_lo, 1)
                        if n == FC + 2 and not last:
                            ln_rstd(s_f_ve, s_f_rstd, g + 2)
                elif not last:
                    ln_rstd(s_f_ve, s_f_rstd, g + 2)
                ln_rstd(s_e_ve, s_e_rstd, g + 1)

            with pool.If(wide > 0):
                groups(pool, ffn, False)
                pool.nop()
            with pool.Else():
                groups(pool, ffn, True)
                pool.nop()

        @block.scalar
        def _(act):
            act.preload_act_table_set("natural_log_exp_and_others")
            act.sem_inc(s_q_out, 2)
            act.sem_inc(s_k_out, 2)

            def high_half(g, t, j):
                act.wait_ge(s_x0T_first, 16) if t is j else act.wait_ge(s_x0T_in, 16 * (G - 1))
                act.activation(xs_hi[:, j], x0T[:, bass.ds(t, 1)].rearrange("p o c s -> p (o c) s"), ACT.Copy).then_inc(s_xs_hi_ok, 1)

            for n, name in enumerate("qkav"):
                c0, cn = COLS[name]
                act.wait_ge(wp_in[n], 16)
                act.activation(wp_hi[:, :, c0:c0 + cn], wp_raw[:, :, c0:c0 + cn], ACT.Copy).then_inc(s_wp_hi_ok, 1)
                if n == 0:
                    for j in range(J):
                        high_half(0, j, j)

            def project(g, last):
                for j in range(J):
                    t, r = g * J + j, j % 2
                    act.wait_ge(s_q_mm, t + 1)
                    act.wait_ge(s_qk_ok, t + 1)
                    act.activation(q_sb[:, r], bank[r * 3][:, :], ACT.Copy).then_inc(s_q_out, 1)
                    act.wait_ge(s_k_mm, t + 1)
                    act.activation(k_sb[:, r], bank[r * 3 + 1][:, :], ACT.Copy).then_inc(s_k_out, 1)
                    act.wait_ge(s_al_out, t + 3)
                    act.wait_ge(s_sp_ok, t + 1)
                    act.activation(sp[:, r], al[:, r], ACT.Abs).then_inc(s_abs_ok, 1)
                    act.wait_ge(s_abs_ok, t + 1)
                    act.activation(sp[:, r], sp[:, r], ACT.Exp, scale=-1.0).then_inc(s_exp_ok, 1)
                    act.wait_ge(s_exp_ok, t + 1)
                    act.activation(sp[:, r], sp[:, r], ACT.Ln, bias=1.0).then_inc(s_ln_ok, 1)
                    if not last:
                        act.wait_ge(s_v_mm, t + 1)
                        high_half(g + 1, t + J, j)
            groups(act, project)

            act.wait_ge(s_wo_in, 16)
            act.activation(wo_hi[:, :, :], wo_raw[:, :, :], ACT.Copy).then_inc(s_wo_hi_ok, 1)
            act.wait_ge(s_tab_d, 2)
            act.activation(decT[:, :], decT[:, :], ACT.Exp).then_inc(s_tab_exp, 1)
            act.activation(betT[:, :], betT[:, :], ACT.Exp).then_inc(s_tab_exp, 1)

            act.wait_ge(s_attn_ready, 1)

            def mix(g):
                for j in range(J):
                    act.wait_ge(s_y_mm, g * J + j + 1)
                    act.activation(vs_hi[:, j], v_sb[:, bass.ds(g * J + j, 1)].rearrange("p o d -> p (o d)"), ACT.Copy).then_inc(s_vhi_ok, 1)
                for j in range(J):
                    act.wait_ge(s_M_ok, g * J + j + 1)
                    act.activation(M_hi[:, j], M_f[:, j], ACT.Copy).then_inc(s_Mhi_ok, 1)
                for j in range(J):
                    act.wait_ge(s_y_mm, g * J + j + 1 + J)
                    act.wait_ge(s_o_mm, g * J + j + 1)
                    act.activation(yT_hi[:, j], bank[j][:, 0:D].rearrange("p (c s) -> p c s", c=DC), ACT.Copy).then_inc(s_yhi_ok, 1)
                for j in range(J):
                    act.wait_ge(s_xn_ok, g * J + j + 1)
                    act.activation(x_tok[:, bass.ds(g * J + j, 1)].rearrange("p o d -> p (o d)"), xn[:, j], ACT.Copy).then_inc(s_xkeep_ok, 1)
                for j in range(J):
                    act.wait_ge(s_xT_mm, g * J + j + 1)
                    act.activation(xT_hi[:, :, bass.ds((g * J + j) * S, S)], bank[j][:, 0:D].rearrange("p (c s) -> p c s", c=DC),
                                   ACT.Copy).then_inc(s_xThi_ok, 1)
            with act.Fori(0, G) as g:
                mix(g)

            def expert_high(e, n):
                act.wait_ge(wx_in[e], n * 16 + 16)
                for c in range(4):
                    a = slice(c * WX // 4, (c + 1) * WX // 4)
                    act.activation(wx_hi[:, e, a], wx_raw[:, e, a], ACT.Copy).then_inc(s_wxhi_ok, 1)
            expert_high(0, 0)
            act.wait_ge(s_o_mm, B + J)
            act.wait_ge(s_xT_mm, B)
            with act.Fori(0, E // 2) as p:
                for u in range(8):
                    for c in range(XC):
                        n = (p * 8 + u) * XC + c
                        act.wait_ge(s_up_mm, n + 1)
                        act.wait_ge(s_down_mm, (p * 8 + u + 1) * J)
                        act.activation(hx_hi[:, u % 2, c], bank[c][:, :], ACT.Relu).then_inc(s_relu_ok, 1)
                    if u == 2:
                        expert_high(1, p)
                    if u == 6:
                        expert_high(0, p + 1)

            act.wait_ge(s_wide_f, 1)
            wide = act.value_load(wide_flag[0:1, 0:1], min_val=0, max_val=1)

            def norm2_T(n0, exact):
                for j in range(J):
                    act.wait_ge(s_f_T, n0 + j + 1)
                    src = bank[4 + j][:, 0:D].rearrange("p (c s) -> p c s", c=DC)
                    dst = (xf_hi if exact else xf_wide)[:, :, j * S:j * S + S]
                    act.activation(dst, src, ACT.Copy).then_inc(s_f_xhi, 1)

            def keep(n0):
                for j in range(J):
                    act.wait_ge(s_f_xn, n0 + j + 1)
                    act.activation(x_tok[:, bass.ds(n0 + j, 1)].rearrange("p o d -> p (o d)"), xn2[:, j], ACT.Copy).then_inc(s_f_keep, 1)

            def ffn(g, last, exact):
                for n in range(3 * FC):
                    layer, m = divmod(n, FC)
                    act.wait_ge(s_f_mm, (g * 3 * FC + n) + 1)
                    if layer == 0:
                        act.wait_ge(s_f_hf, g * FC + m + 1)
                        act.activation(silu[:, m % 2], bank[2 * (m % 2)][:, :], ACT.Silu, scale=scales[:, 0, m:m + 1]).then_inc(s_f_silu, 1)
                    else:
                        b = bank[m % 4]
                        if exact:
                            act.wait_ge(s_f_lo, g * 3 * FC + n + 1)
                            act.activation(hf[:, n % 3], b[:, :], ACT.Gelu, scale=scales[:, 1 + layer, m:m + 1]).then_inc(s_l_out, 1)
                        else:
                            dst = [hb_wide, ha_wide][layer - 1]
                            act.activation(dst[:, m], b[:, :], ACT.Gelu, scale=scales[:, 1 + layer, m:m + 1]).then_inc(s_l_out, 1)
                    if n == 2 * FC - 1 and not last:
                        keep((g + 1) * J)
                        norm2_T((g + 1) * J, exact)

            with act.If(wide > 0):
                keep(0)
                norm2_T(0, False)
                groups(act, ffn, False)
                act.nop()
            with act.Else():
                keep(0)
                norm2_T(0, True)
                groups(act, ffn, True)
                act.nop()

        @block.tensor
        def _(pe):

            def product(dst, pairs, inc=None):
                for n, (a, b) in enumerate(pairs):
                    mm = pe.matmul(dst, a, b, start=(n == 0), stop=(n == len(pairs) - 1))
                if inc is not None:
                    mm.then_inc(inc, 1)
                return mm

            def three(a_hi, a_lo, b_hi, b_lo):
                return [(a_hi, b_hi), (a_hi, b_lo), (a_lo, b_hi)]

            def project(g, last):
                for j in range(J):
                    t, r = g * J + j, j % 2
                    pe.wait_ge(s_xs_lo_ok, t + 1)
                    for n, name in enumerate("qkav"):
                        c0, cn = COLS[name]
                        pe.wait_ge(s_wp_lo_ok, n + 1)
                        pe.wait_ge((s_q_out, s_k_out, s_al_out, s_v_out)[n], t + 1)
                        dst = bank[6][:, 0:D] if name == "v" else bank[r * 3 + n][:, :]
                        product(dst, [pair for c in range(DC) for pair in three(
                            xs_hi[:, j, c], xs_lo[:, j, c], wp_hi[:, c, c0:c0 + cn], wp_lo[:, c, c0:c0 + cn])],
                            (s_q_mm, s_k_mm, s_a_mm, s_v_mm)[n])
                    if j % 2 == 1:
                        e = g * 2 + j // 2
                        pe.wait_ge(s_mask_ok, e + 1)
                        for b in range(B):
                            mm = pe.matmul(bank[7][:, bass.ds(e * B + b, 1)], mask[:, j // 2, b], ones, start=True, stop=True)
                        mm.then_inc(s_gate_mm, 1)
            ones = expert_no[:, 1:2]
            pe.wait_ge(s_const_ok, 3)
            pe.wait_ge(s_wp_hi_ok, 4)
            groups(pe, project)

            pe.wait_ge(s_sp_ok, B + 2)
            pe.wait_ge(s_b_red, B + 2)
            pe.wait_ge(s_q_out, B + 2)
            pe.wait_ge(s_k_out, B + 2)
            pe.transpose(bank[0][:, 0:P], b_tok[:, :, :].rearrange("p b h -> p (b h)"), ident[:, :]).then_inc(s_ba_T, 1)
            pe.transpose(bank[1][:, 0:P], a_tok[:, :, :].rearrange("p b h -> p (b h)"), ident[:, :]).then_inc(s_ba_T, 1)
            pe.wait_ge(s_chain, 8)
            pe.transpose(bank[2][:, 0:P], BT[:, :], ident[:, :]).then_inc(s_B_T, 1)
            pe.wait_ge(s_attn_ready, 1)
            pe.wait_ge(s_wo_lo_ok, 1)

            def mix(g):
                for j in range(J):
                    t = g * J + j
                    pe.wait_ge(s_Mlo_ok, t + 1)
                    pe.wait_ge(s_vlo_ok, t + 1)
                    pe.wait_ge(s_xTlo_ok, t + 1)
                    for c in range(DC):
                        a = slice(c * P, c * P + P)
                        mm = product(bank[j][:, a], three(vs_hi[:, j, a], vs_lo[:, j, a], M_hi[:, j], M_lo[:, j]))
                    mm.then_inc(s_y_mm, 1)
                for j in range(J):
                    t = g * J + j
                    pe.wait_ge(s_ylo_ok, t + 1)
                    pe.wait_ge(s_res_ok, t + 1)
                    product(bank[4 + j][:, 0:D], [pair for c in range(DC) for pair in three(
                        yT_hi[:, j, c], yT_lo[:, j, c], wo_hi[:, c], wo_lo[:, c])], s_o_mm)
                for j in range(J):
                    pe.wait_ge(s_xn_ok, g * J + j + 1)
                    pe.transpose(bank[j][:, 0:P], xn[:, j, 0:P], ident[:, :])
                    pe.transpose(bank[j][:, P:2 * P], xn[:, j, P:2 * P], ident[:, :]).then_inc(s_xT_mm, 1)
            pe.sem_inc(s_y_mm, J)
            pe.sem_inc(s_o_mm, J)
            with pe.Fori(0, G) as g:
                mix(g)

            pe.wait_ge(s_xTlo_ok, B + J)
            pe.wait_ge(s_res_ok, B + J)

            def up(p, u):
                e, g = divmod(u, G)
                pe.wait_ge(s_wxlo_ok, (p * 2 + e) * 4 + 4)
                wi_hi = wx_hi[:, e, 0:DC * DX].rearrange("p (c d) -> p c d", c=DC)
                wi_lo = wx_lo[:, e, 0:DC * DX].rearrange("p (c d) -> p c d", c=DC)
                for c in range(XC):
                    pe.wait_ge(s_hlo_ok, (p * 8 + u) * XC + c + 1)
                    a = slice(c * P, c * P + P)
                    product(bank[c][:, :], [pair for i in range(DC) for pair in three(
                        wi_hi[:, i, a], wi_lo[:, i, a], xT_hi[:, i, g * N:g * N + N], xT_lo[:, i, g * N:g * N + N])], s_up_mm)

            def down(p, u):
                e, g = divmod(u, G)
                wo_h = wx_hi[:, e, DC * DX:WX].rearrange("p (c d) -> p c d", c=XC)
                wo_l = wx_lo[:, e, DC * DX:WX].rearrange("p (c d) -> p c d", c=XC)
                for j in range(J):
                    n = (p * 8 + u) * J + j
                    pe.wait_ge(s_gated_ok, n + 1)
                    a = slice(j * S, j * S + S)
                    pairs = []
                    for c in range(XC):
                        if j == 0:
                            pairs.append(None)
                        pairs += three(hx_hi[:, u % 2, c, a], hx_lo[:, u % 2, c, a], wo_h[:, c], wo_l[:, c])
                    dst, first, left = bank[4 + j][:, 0:D], True, sum(q is not None for q in pairs)
                    c = 0
                    for q in pairs:
                        if q is None:
                            pe.wait_ge(s_hlo_ok, (p * 8 + u) * XC + c + 1 + XC)
                            c += 1
                            continue
                        left -= 1
                        mm = pe.matmul(dst, q[0], q[1], start=first, stop=(left == 0))
                        first = False
                    mm.then_inc(s_down_mm, 1)

            pe.sem_inc(s_down_mm, 2 * J)
            with pe.Fori(0, E // 2) as p:
                up(p, 0)
                for u in range(8):
                    if u < 7:
                        up(p, u + 1)
                    down(p, u)

            pe.wait_ge(s_wide_f, 1)
            wide = pe.value_load(wide_flag[0:1, 0:1], min_val=0, max_val=1)

            def norm2_T(n0):
                for j in range(J):
                    pe.wait_ge(s_f_xn, n0 + j + 1)
                    pe.transpose(bank[4 + j][:, 0:P], xn2[:, j, 0:P], ident[:, :])
                    pe.transpose(bank[4 + j][:, P:2 * P], xn2[:, j, P:2 * P], ident[:, :]).then_inc(s_f_T, 1)

            W1, W2, H1, H2, W3 = 0, DC * F, 2 * DC * F, 2 * DC * F + FC * F, 2 * DC * F + 2 * FC * F

            def ffn(g, last, exact):
                wf = wf_hi if exact else wf_raw
                x_parts = [xf_hi, xf_lo] if exact else [xf_wide]
                a_parts = [ha_hi, ha_lo] if exact else [ha_wide]
                b_parts = [hb_hi, hb_lo] if exact else [hb_wide]
                pe.wait_ge(s_f_xlo if exact else s_f_xhi, g * J + J)
                for m in range(FC):
                    r = 2 * (m % 2)
                    for o, b in ((W1, r), (W2, r + 1)):
                        pe.wait_ge(s_f_hf, g * FC + m + 1)
                        mm = product(bank[b][:, :], [(wf[:, o + c * F + m * P:o + c * F + m * P + P], part[:, c])
                                                     for c in range(DC) for part in x_parts])
                    mm.then_inc(s_f_mm, 1)
                for layer, (o, parts) in enumerate(((H1, a_parts), (H2, b_parts))):
                    for m in range(FC):
                        n = (layer + 1) * FC + m
                        if m < 4:
                            pe.wait_ge(s_f_hf, g * FC + FC + 2) if layer == 0 else pe.wait_ge(s_l_out, (g * 2 + layer) * FC - 4 + m + 1)
                        else:
                            pe.wait_ge(s_l_out, (g * 2 + layer) * FC + m - 4 + 1)
                        for k in range(FC):
                            if m == 0:
                                if exact:
                                    pe.wait_ge(s_f_lo, g * 3 * FC + layer * FC + k + 4)
                                elif layer == 0:
                                    pe.wait_ge(s_f_hf, g * FC + k + 3)
                                else:
                                    pe.wait_ge(s_l_out, g * 2 * FC + k + 1)
                            for i, part in enumerate(parts):
                                mm = pe.matmul(bank[m % 4][:, :], wf[:, o + k * F + m * P:o + k * F + m * P + P], part[:, k],
                                               start=(k == 0 and i == 0), stop=(k == FC - 1 and i == len(parts) - 1))
                        mm.then_inc(s_f_mm, 1)
                    if layer == 0 and not last:
                        pe.wait_ge(s_e_mul, g * J + 1)
                        norm2_T((g + 1) * J)
                for j in range(J):
                    if j == 0:
                        if exact:
                            pe.wait_ge(s_f_lo, g * 3 * FC + 3 * FC + 3)
                        else:
                            pe.wait_ge(s_l_out, g * 2 * FC + 2 * FC)
                        if not last:
                            pe.wait_ge(s_f_xlo if exact else s_f_xhi, (g + 2) * J)
                    a = slice(j * S, j * S + S)
                    product(bank[4 + j][:, 0:D], [(part[:, k, a], wf[:, W3 + k * D:W3 + k * D + D])
                                                  for k in range(FC) for part in a_parts], s_e_y)

            with pe.If(wide > 0):
                pe.wait_ge(s_raw_in, 16)
                norm2_T(0)
                groups(pe, ffn, False)
                pe.nop()
            with pe.Else():
                norm2_T(0)
                groups(pe, ffn, True)
                pe.nop()

        @block.vector
        def _(dve):
            dve.sem_inc(s_al_out, 2)
            dve.sem_inc(s_v_out, 1)
            dve.sem_inc(s_b_red, 2)
            dve.sem_inc(s_qk_ok, 2)
            dve.sem_inc(s_sp_ok, 2)
            for n, name in enumerate("qkav"):
                c0, cn = COLS[name]
                dve.wait_ge(s_wp_hi_ok, n + 1)
                dve.tensor_tensor(wp_lo[:, :, c0:c0 + cn], wp_raw[:, :, c0:c0 + cn], wp_hi[:, :, c0:c0 + cn].bitcast(F32),
                                  ALU.subtract).then_inc(s_wp_lo_ok, 1)
            dve.wait_ge(s_bias_in, 16)
            dve.wait_ge(s_gate_in, 32)
            dve.wait_ge(s_const_ok, 3)

            def project(g, last):
                for j in range(J):
                    t, r = g * J + j, j % 2
                    dve.wait_ge(s_a_mm, t + 1)
                    dve.tensor_tensor(al[:, r], bank[r * 3 + 2][:, :], bias_b[:, :], ALU.add).then_inc(s_al_out, 1)
                    dve.wait_ge(s_v_mm, t + 1)
                    dve.tensor_scalar(sgn[:, :], bank[6][:, 0:D], 0.0, 2 * EPS, ALU.is_ge, ALU.mult).then_inc(s_sgn_ok, 1)
                    dve.wait_ge(s_sgn_ok, t + 1)
                    dve.scalar_tensor_tensor(out=v_sb[:, bass.ds(t, 1)].rearrange("p o d -> p (o d)"), in0=sgn[:, :], scalar=EPS,
                                             in1=bank[6][:, 0:D], op0=ALU.subtract, op1=ALU.add).then_inc(s_v_out, 1)
                    if j % 2 == 0:
                        e = g * 2 + j // 2
                        dve.wait_ge(s_gate_mm, e + 1)
                        dve.scalar_tensor_tensor(out=mask[:, j // 2].rearrange("p b s -> p (b s)"),
                                                 in0=itok_sb[:, :, :].rearrange("p b s -> p (b s)"), scalar=expert_no[:, bass.ds(e, 1)],
                                                 in1=ctx_sb[:, :, :].rearrange("p b s -> p (b s)"),
                                                 op0=ALU.is_equal, op1=ALU.mult).then_inc(s_mask_ok, 1)
                    dve.wait_ge(s_ln_ok, t + 1)
                    dve.scalar_tensor_tensor(out=sp[:, r], in0=al[:, r], scalar=0.0, in1=sp[:, r], op0=ALU.max,
                                             op1=ALU.add).then_inc(s_sp_sum, 1)
                    dve.wait_ge(s_qk_ok, t + 3)
                    dve.tensor_reduce(b_tok[:, bass.ds(t, 1)].rearrange("p o h -> p (o h)"), qk[:, r].rearrange("p (h d) -> p h d", h=H),
                                      AX_X, ALU.add).then_inc(s_b_red, 1)
                    dve.wait_ge(s_sp_sum, t + 1)
                    dve.tensor_reduce(a_tok[:, bass.ds(t, 1)].rearrange("p o h -> p (o h)"), sp[:, r].rearrange("p (h d) -> p h d", h=H),
                                      AX_X, ALU.add).then_inc(s_sp_ok, 1)
            dve.sem_inc(s_gate_mm, 2)
            groups(dve, project)

            chain = [0]

            def link(instruction):
                instruction.then_inc(s_chain, 1)
                chain[0] += 1
                dve.wait_ge(s_chain, chain[0])

            dve.wait_ge(s_sp_ok, B + 2)
            dve.wait_ge(s_ba_T, 2)
            dve.tensor_scalar(bT[:, :], bank[0][:, 0:S], SCALE, None, ALU.mult)
            link(dve.tensor_scalar(aT[:, :], bank[1][:, 0:S], -1.0, None, ALU.mult))
            link(dve.memset(aT[:, 0:1], 0.0))
            link(dve.tensor_tensor_scan(mT[:, :], aT[:, :], bT[:, :], LOWEST, ALU.add, ALU.max))
            dve.tensor_tensor(betT[:, :], bT[:, :], mT[:, :], ALU.subtract).then_inc(s_tab_d, 1)
            link(dve.tensor_tensor(decT[:, 1:S], aT[:, 1:S], mT[:, 0:S - 1], ALU.add))
            dve.memset(decT[:, 0:1], 0.0)
            dve.tensor_tensor(decT[:, 1:S], decT[:, 1:S], mT[:, 1:S], ALU.subtract).then_inc(s_tab_d, 1)
            dve.wait_ge(s_tab_exp, 2)
            link(dve.memset(decT[:, 0:1], 0.0))
            link(dve.tensor_tensor_scan(eT[:, :], decT[:, :], betT[:, :], 0.0, ALU.mult, ALU.add))
            link(dve.reciprocal(rT[:, :], eT[:, :]))
            link(dve.tensor_tensor(BT[:, :], betT[:, :], rT[:, :], ALU.mult))
            dve.memset(AT[:, 0:1], 0.0)
            link(dve.tensor_tensor(AT[:, 1:S], decT[:, 1:S], eT[:, 0:S - 1], ALU.mult))
            dve.tensor_tensor(AT[:, :], AT[:, :], rT[:, :], ALU.mult).then_inc(s_A_ok, 1)
            v_all = v_sb[:, :, :].rearrange("p b d -> p (b d)")
            link(dve.scalar_tensor_tensor(out=junk[:, :], in0=v_all, scalar=-1.0, in1=v_all, op0=ALU.mult, op1=ALU.max))
            dve.tensor_reduce(vstat[:, 0:1], junk[:, :], AX_X, ALU.max).then_inc(s_vstat_ok, 1)
            link(dve.tensor_reduce(vstat[:, 1:2], junk[:, :], AX_X, ALU.min))
            dve.tensor_scalar(vstat[:, 1:2], vstat[:, 1:2], -1.0, None, ALU.mult).then_inc(s_vstat_ok, 1)
            dve.wait_ge(s_B_T, 1)
            dve.tensor_copy(B_tok[:, :], bank[2][:, 0:S]).then_inc(s_BtokOK, 1)
            dve.wait_ge(s_vall_ok, 1)
            dve.wait_ge(s_A_ok, 1)
            link(dve.tensor_scalar(val[:, :], BT[:, :], vall[:, 1:2], None, ALU.mult))
            link(dve.tensor_scalar(vall[:, 0:1], vall[:, 0:1], 2.01, None, ALU.mult))
            link(dve.scalar_tensor_tensor(out=val[:, :], in0=AT[:, :], scalar=vall[:, 0:1], in1=val[:, :],
                                          op0=ALU.mult, op1=ALU.add))
            dve.tensor_reduce(cond[:, :], val[:, :], AX_X, ALU.max).then_inc(s_cond_ok, 1)
            dve.wait_ge(s_condall_ok, 1)
            dve.tensor_scalar(flag[:, :], cond_all[:, :], 0.0, None, ALU.is_gt).then_inc(s_flag_ok, 1)
            dve.wait_ge(s_wo_hi_ok, 1)
            dve.tensor_tensor(wo_lo[:, :, :], wo_raw[:, :, :], wo_hi[:, :, :].bitcast(F32), ALU.subtract).then_inc(s_wo_lo_ok, 1)
            dve.wait_ge(s_gate_mm, E + 2)
            dve.tensor_copy(gates[:, :, :].rearrange("p b e -> p e b"), bank[7][:, 0:B * E].rearrange("p (e b) -> p e b", e=E)
                            ).then_inc(s_gates_ok, 1)
            dve.wait_ge(s_flag_ok, 1)
            dve.wait_ge(s_BtokOK, 1)
            stepwise = dve.value_load(flag[0:1, 0:1], min_val=0, max_val=1)
            with dve.If(stepwise > 0):
                step_path(dve)
                dve.nop()
            with dve.Else():
                dve.nop()
            dve.sem_inc(s_res_ok, J)
            dve.sem_inc(s_xTlo_ok, J)
            dve.sem_inc(s_scan_ok, J)
            dve.wait_ge(s_xtok_in, 16)
            dve.memset(cond[:, :], 0.0).then_inc(s_attn_ready, 1)

            def mix(g):
                for j in range(J):
                    t = g * J + j
                    dve.wait_ge(abc_in[j], 16 * g + 16)
                    dve.tensor_tensor_scan(decay[:, j], a_bc[:, j], ident8[:, :], 0.0, ALU.mult, ALU.add).then_inc(s_scan_ok, 1)
                for j in range(J):
                    t = g * J + j
                    dve.wait_ge(s_wB_ok, t + 1)
                    dve.tensor_reduce(M_f[:, j], decay[:, j].rearrange("p (h s) -> p s h", h=H), AX_X, ALU.add).then_inc(s_M_ok, 1)
                for j in range(J):
                    dve.wait_ge(s_yhi_ok, g * J + j + 1)
                    dve.tensor_tensor(yT_lo[:, j], bank[j][:, 0:D].rearrange("p (c s) -> p c s", c=DC), yT_hi[:, j].bitcast(F32),
                                      ALU.subtract).then_inc(s_ylo_ok, 1)
                for j in range(J):
                    t = g * J + j
                    dve.wait_ge(s_o_mm, t + 1 + J)
                    row = x_tok[:, bass.ds(t, 1)].rearrange("p o d -> p (o d)")
                    dve.tensor_tensor(row, bank[4 + j][:, 0:D], row, ALU.add).then_inc(s_res_ok, 1)
                norm_rows(g * J, lambda j: x_tok[:, bass.ds(g * J + j, 1)].rearrange("p o d -> p (o d)"), xn, g,
                          s_res_ok, J, s_bn_ok, s_mv_ok, s_ve_ok, s_rstd_ok, s_xn_ok)
                for j in range(J):
                    t = g * J + j
                    dve.wait_ge(s_xThi_ok, t + 1)
                    cols = bass.ds(t * S, S)
                    dve.tensor_tensor(xT_lo[:, :, cols], bank[j][:, 0:D].rearrange("p (c s) -> p c s", c=DC),
                                      xT_hi[:, :, cols].bitcast(F32), ALU.subtract).then_inc(s_xTlo_ok, 1)

            def norm_rows(n0, row, dst, g, have, extra, stats, means, var, root, normed):
                for j in range(J):
                    if have is not None:
                        dve.wait_ge(have, n0 + j + 1 + extra)
                        dve.sem_inc(s_bn_tick, 1)
                    dve.bn_stats(bn[:, j], row(j)).then_inc(stats, 1)
                for j in range(J):
                    dve.wait_ge(stats, n0 + j + 1)
                    dve.sem_inc(s_bn_tick, 1)
                    dve.bn_aggr(mv[:, j], bn[:, j]).then_inc(means, 1)
                dve.wait_ge(means, n0 + J)
                dve.tensor_scalar(var_eps[:, :], mv[:, :, 1], LN_EPS, None, ALU.add).then_inc(var, 1)
                dve.wait_ge(root, g + 1)
                for j in range(J):
                    dve.tensor_scalar(dst[:, j], row(j), mv[:, j, 0:1], rstd[:, j:j + 1], ALU.subtract, ALU.mult).then_inc(normed, 1)

            with dve.Fori(0, G) as g:
                mix(g)

            dve.sem_inc(s_hlo_ok, XC)
            dve.sem_inc(s_gated_ok, J)
            dve.sem_inc(s_stage_used, 2)

            def low(p, u):
                for c in range(XC):
                    n = (p * 8 + u) * XC + c
                    dve.wait_ge(s_relu_ok, n + 1)
                    dve.scalar_tensor_tensor(out=hx_lo[:, u % 2, c], in0=bank[c][:, :], scalar=0.0, in1=hx_hi[:, u % 2, c].bitcast(F32),
                                             op0=ALU.max, op1=ALU.subtract).then_inc(s_hlo_ok, 1)

            def gated(p, u):
                e, g = divmod(u, G)
                for j in range(J):
                    dve.wait_ge(s_down_mm, (p * 8 + u) * J + j + 1 + 2 * J)
                    dve.wait_ge(s_gated_ok, (p * 8 + u) * J + j + 1)
                    row = x_tok[:, g * J + j]
                    dve.scalar_tensor_tensor(out=row, in0=bank[4 + j][:, 0:D], scalar=gates[:, g * J + j, bass.ds(p * 2 + e, 1)],
                                             in1=row, op0=ALU.mult, op1=ALU.add).then_inc(s_gated_ok, 1)

            def take_piece(p, u):
                n = p * 8 + u
                dve.wait_ge(stage_in[u % 2], (p * 4 + u // 2) * 16 + 16)
                dve.tensor_copy(wf_hi[:, bass.ds(n * CH, CH)], stage[:, u % 2]).then_inc(s_st_cmp, 1)
                dve.wait_ge(s_st_cmp, n + 1)
                dve.scalar_tensor_tensor(out=stage[:, u % 2], in0=stage[:, u % 2], scalar=1.0, in1=wf_hi[:, bass.ds(n * CH, CH)].bitcast(F32),
                                         op0=ALU.mult, op1=ALU.not_equal, accum_out=neq[:, bass.ds(n, 1)]).then_inc(s_stage_used, 1)

            dve.wait_ge(s_Mlo_ok, B)
            with dve.Fori(0, E // 2) as p:
                low(p, 0)
                for u in range(8):
                    if u < 7:
                        low(p, u + 1)
                    take_piece(p, u)
                    gated(p, u)

            dve.wait_ge(s_stage_used, 34)
            dve.tensor_reduce(wide_col[:, :], neq[:, :], AX_X, ALU.max).then_inc(s_wide_c, 1)
            dve.wait_ge(s_wide_a, 1)
            dve.tensor_scalar(wide_flag[:, :], wide_all[:, :], 0.0, None, ALU.is_gt).then_inc(s_wide_f, 1)

            def norm2(n0, g, first=False):
                norm_rows(n0, lambda j: x_tok[:, bass.ds(n0 + j, 1)].rearrange("p o d -> p (o d)"), xn2, g,
                          None, 0, s_f_bn, s_f_mv, s_f_ve, s_f_rstd, s_f_xn)

            def norm2_low(n0):
                for j in range(J):
                    dve.wait_ge(s_f_xhi, n0 + j + 1)
                    src = bank[4 + j][:, 0:D].rearrange("p (c s) -> p c s", c=DC)
                    cols = slice(j * S, j * S + S)
                    dve.tensor_tensor(xf_lo[:, :, cols], src, xf_hi[:, :, cols].bitcast(F32), ALU.subtract).then_inc(s_f_xlo, 1)

            dve.wait_ge(s_gated_ok, B * E + J)
            norm2(0, 0)
            dve.sem_inc(s_f_hf, 2)
            dve.sem_inc(s_f_lo, 3)
            dve.sem_inc(s_e_mul, 1)
            dve.wait_ge(s_wide_f, 1)
            wide = dve.value_load(wide_flag[0:1, 0:1], min_val=0, max_val=1)
            dve.wait_ge(s_s3_in, 16)
            dve.wait_ge(s_small_in, 16)

            def ffn(g, last, exact):
                for n in range(3 * FC):
                    layer, m = divmod(n, FC)
                    dst = [ha_hi, hb_hi, ha_hi][layer]
                    if layer == 0:
                        dve.wait_ge(s_f_silu, g * FC + m + 1)
                        if exact:
                            dve.wait_ge(s_f_lo, g * 3 * FC + n + 1)
                            o = hf[:, n % 3]
                        else:
                            o = ha_wide[:, m]
                        dve.scalar_tensor_tensor(out=o, in0=bank[2 * (m % 2) + 1][:, :], scalar=scales[:, 1, m:m + 1], in1=silu[:, m % 2],
                                                 op0=ALU.mult, op1=ALU.mult).then_inc(s_f_hf, 1)
                        if exact:
                            dve.wait_ge(s_f_hf, g * FC + m + 3)
                    elif exact:
                        dve.wait_ge(s_l_out, g * 2 * FC + (layer - 1) * FC + m + 1)
                    if exact:
                        dve.tensor_copy(dst[:, m], hf[:, n % 3]).then_inc(s_f_hi, 1)
                    if n == FC + 2 and not last:
                        norm2((g + 1) * J, g + 1)
                    if n == 2 * FC + 1 and not last and exact:
                        norm2_low((g + 1) * J)
                for j in range(J):
                    t = g * J + j
                    dve.wait_ge(s_e_y, t + 1)
                    dve.tensor_tensor(y_s[:, j % 2], bank[4 + j][:, 0:D], s3_b[:, :], ALU.mult).then_inc(s_e_mul, 1)
                    dve.wait_ge(s_e_mul, t + 2)
                    row = x_tok[:, bass.ds(t, 1)].rearrange("p o d -> p (o d)")
                    dve.tensor_tensor(row, y_s[:, j % 2], row, ALU.add).then_inc(s_e_add, 1)
                for j in range(J):
                    dve.wait_ge(out_done[j], 16 * g + 16)
                norm_rows(g * J, lambda j: x_tok[:, bass.ds(g * J + j, 1)].rearrange("p o d -> p (o d)"), xo, g,
                          s_e_add, 0, s_e_bn, s_e_mv, s_e_ve, s_e_rstd, s_e_xo)

            for j in range(J):
                dve.sem_inc(out_done[j], 16)
            with dve.If(wide > 0):
                groups(dve, ffn, False)
                dve.nop()
            with dve.Else():
                norm2_low(0)
                groups(dve, ffn, True)
                dve.nop()


def tiled(w, chunks):
    return np.ascontiguousarray(np.asarray(w).T.reshape(chunks, P, -1).transpose(1, 0, 2))


def laid_out(i):
    a = {k: np.asarray(v) for k, v in i.items()}
    words = lambda *ws: np.ascontiguousarray(np.concatenate([w.reshape(P, -1) for w in ws], axis=1))
    return {
        "x": np.ascontiguousarray(a["x"]),
        "xT": np.ascontiguousarray(a["x"].reshape(B, S, DC, P).transpose(3, 0, 2, 1)),
        "wproj": np.concatenate([tiled(a["L0_attn_" + n], DC) for n in ("W_q", "W_k", "W_alpha_w", "W_v")], axis=2),
        "wo": tiled(a["L0_attn_W_o"], DC),
        "alpha_b": np.ascontiguousarray(a["L0_attn_W_alpha_b"]),
        "ctx": np.ascontiguousarray(a["ctx_512"]),
        "itok": np.ascontiguousarray(a["itok_BxS2xS_0_7"]),
        "wx": np.stack([words(tiled(a["L0_xattn_proj_in"][e], DC), tiled(a["L0_xattn_proj_out"][e], XC)) for e in range(E)]),
        "wffn": words(tiled(a["L0_ffn_w1_w"], DC), tiled(a["L0_ffn_w2_w"], DC), tiled(a["L0_ffn_h1_w"], FC),
                      tiled(a["L0_ffn_h2_w"], FC), tiled(a["L0_ffn_w3_w"], FC)),
        "ffn_s": np.ascontiguousarray(np.stack([a["L0_ffn_" + n].reshape(FC, P).T for n in ("w1_s", "w2_s", "h1_s", "h2_s")], axis=1)),
        "w3_s": np.ascontiguousarray(a["L0_ffn_w3_s"]),
    }


def kernel(**inputs):
    import concourse.bacc as bacc
    from concourse.bass_utils import run_bass_kernel_spmd

    nc = bacc.Bacc("TRN2", target_bir_lowering=False, num_devices=1)
    arrays, args = {}, []
    for name, array in laid_out(inputs).items():
        arrays[f"in_{name}"] = array
        args.append(nc.dram_tensor(f"in_{name}", array.shape, mybir.dt.from_np(array.dtype), kind="ExternalInput").ap())
    args.append(nc.dram_tensor("out_0", (B, S, D), F32, kind="ExternalOutput").ap())
    decoder_kernel(nc, *args)
    return run_bass_kernel_spmd(nc, [arrays], core_ids=[0]).results[0]["out_0"]
```

```python
import math
from contextlib import ExitStack

import numpy as np

import concourse.bass as bass
from concourse import mybir

F32 = mybir.dt.float32
F32R = mybir.dt.float32r
I32 = mybir.dt.int32
ALU = mybir.AluOpType
ACT = mybir.ActivationFunctionType
AX_X = mybir.AxisListType.X
RMAX = bass.bass_isa.ReduceOp.max

P = 128
B, S, D = 16, 128, 256
H, DH = 8, 64
HD = H * DH
E, DX = 8, 512
F = 1024
DC, XC, FC = D // P, DX // P, F // P
J = 4
G = B // J
N = J * S
WP = 3 * HD + D
WX = DC * DX + XC * D
WF = 2 * DC * F + 2 * FC * F + FC * D
PIECE = 512
LN_EPS = 1e-5
EPS = 1e-8
SCALE = 1.0 / math.sqrt(DH)
LOWEST = -3.0e38
PIECES = WF // PIECE
assert S == P and B * H == P and WF % PIECE == 0 and PIECES == 2 * (2 * 8 + 6)




def decoder_kernel(nc, x, xT, wproj, wo, alpha_b, ctx, itok, wx, wffn, ffn_s, w3_s, out):
    with ExitStack() as stack:
        base = [16512]

        def region(nbytes):
            at = base[0]
            base[0] += nbytes
            return at

        def at(name, offset, shape, dt=F32):
            return nc.alloc_sbuf_tensor_at(name, [P, *shape], dt, offset=offset)

        def at_r(name, offset, shape):
            return at(name, offset, shape, F32R)

        def both(name, offset, shape):
            return at(name + "_r", offset, shape, F32R), at(name + "_f", offset, shape)

        def sem(name):
            return stack.enter_context(nc.semaphore(name))

        o_x, o_xh, o_xl = region(B * D * 4), region(B * D * 4), region(B * D * 4)
        o_w, o_ha, o_hb = region(WF * 4), region(2 * FC * N * 4), region(2 * FC * N * 4)

        x_tok = at("x_tok", o_x, [B, D])
        xT_hi = at_r("xT_hi", o_xh, [DC, B * S])
        xT_lo = at_r("xT_lo", o_xl, [DC, B * S])
        def small(name, shape, dt=F32):
            return at(name, region(-(-4 * math.prod(shape) // 32) * 32), shape, dt)

        gates, ident, scales, neq = small("gates", [B, E]), small("ident", [P]), small("scales", [4, FC]), small("neq", [PIECES])
        expert_no = small("expert_no", [E])
        bn, mv, var_eps = small("bn", [J, 6]), small("mv", [J, 2]), small("var_eps", [J])
        rstd, neghalf = small("rstd", [J]), small("neghalf", [J])
        extremes, extreme, products = small("extremes", [3]), small("extreme", [3]), small("products", [2])
        wide_col, wide_all = small("wide_col", [1]), small("wide_all", [1])
        flag, wide_flag = small("flag", [1], I32), small("wide_flag", [1], I32)
        stage = small("stage", [2, PIECE])
        assert base[0] <= 229344

        x0T = at("x0T", o_xl, [B, DC, S])
        wp_hi = at_r("wp_hi", o_w, [DC, WP])
        wp_lo, wp_raw = both("wp_lo", o_w + 14336, [DC, WP])
        wo_hi = at_r("wo_hi", o_w + 28672, [DC, D])
        wo_lo, wo_raw = both("wo_lo", o_w + 30720, [DC, D])
        v_sb = at("v_sb", o_w + 32768, [B, D])
        bias_b = at("bias_b", o_w + 49152, [HD])
        q_sb = at("q_sb", o_w + 51200, [2, HD])
        k_sb = at("k_sb", o_w + 55296, [2, HD])
        qk = at("qk", o_w + 59392, [2, HD])
        al = at("al", o_w + 63488, [2, HD])
        sp = at("sp", o_w + 67584, [2, HD])
        ctx_sb = at("ctx_sb", o_w + 71680, [B, S])
        itok_sb = at("itok_sb", o_w + 79872, [B, S], I32)
        masked, masked_late = at("masked", o_ha, [4, S]), at("masked_late", o_w + 67584, [4, S])
        xs_hi = at_r("xs_hi", o_ha + 16384, [J, DC, S])
        xs_lo = at_r("xs_lo", o_ha + 20480, [J, DC, S])
        b_tok = at("b_tok", o_ha + 24576, [B, H])
        a_tok = at("a_tok", o_ha + 25088, [B, H])
        sgn = at("sgn", o_ha + 25600, [D])
        v_size, v_sizes = at("v_size", o_ha + 26624, [2, D]), at("v_sizes", o_ha + 28672, [B])
        bT, aT, mT, decT, betT, eT, rT, BT, AT, B_tok, val = (
            at(n, o_w + 65536 + 512 * i, [S]) for i, n in enumerate(
                ["bT", "aT", "mT", "decT", "betT", "eT", "rT", "BT", "AT", "B_tok", "val"]))
        M_f = at("M_f", o_w + 51200, [J, S])
        M_hi = at_r("M_hi", o_w + 53248, [J, S])
        M_lo = at_r("M_lo", o_w + 55296, [J, S])
        vs_hi = at_r("vs_hi", o_w + 57344, [J, D])
        vs_lo = at_r("vs_lo", o_w + 61440, [J, D])
        decay = at("decay", o_w + 71680, [J, H * S])
        a_bc = at("a_bc", o_w, [J, H * S])
        yT_hi = at_r("yT_hi", o_w + 16384, [J, DC, S])
        yT_lo = at_r("yT_lo", o_w + 20480, [J, DC, S])
        xn = at("xn", o_w + 24576, [J, D])
        r_now, v_now, n_now, raw_now, mx_now, sg_now = (
            at(n, o_w + 71680 + 1024 * i, [D]) for i, n in enumerate(
                ["r_now", "v_now", "n_now", "raw_now", "mx_now", "sg_now"]))
        r_heads = at("r_heads", o_w + 79872, [H, D])
        wx_hi = at_r("wx_hi", o_hb, [2, WX])
        wx_lo, wx_raw = both("wx_lo", o_hb + 2 * WX * 4, [2, WX])
        hx_hi = at_r("hx_hi", o_ha, [2, XC, N])
        hx_lo = at_r("hx_lo", o_ha + 2 * XC * N * 4, [2, XC, N])
        wf_hi, wf_raw = both("wf_hi", o_w, [WF])
        xf_hi, xf_wide = both("xf_hi", o_xh, [DC, N])
        xf_lo = at_r("xf_lo", o_xh + 4096, [DC, N])
        s3_b = at("s3_b", o_xh + 8192, [D])
        y_s = at("y_s", o_xh + 9216, [2, D])
        xo = at("xo", o_xh + 12288, [J, D])
        silu = at("silu", o_xl, [2, N])
        hf = at("hf", o_xl + 4096, [3, N])
        xn2 = at("xn2", o_xl + 10240, [J, D])
        ha_hi, ha_wide = both("ha_hi", o_ha, [FC, N])
        ha_lo = at_r("ha_lo", o_ha + FC * N * 4, [FC, N])
        hb_hi, hb_wide = both("hb_hi", o_hb, [FC, N])
        hb_lo = at_r("hb_lo", o_hb + FC * N * 4, [FC, N])

        bank = [stack.enter_context(nc.psum_tensor(f"bank{i}", [P, 512], F32)) for i in range(8)]

        a_dram = nc.dram_tensor("a_dram", (P, S), F32, kind="Internal").ap()
        v_dram = nc.dram_tensor("v_dram", (B, S, D), F32, kind="Internal").ap()
        r_dram = nc.dram_tensor("r_dram", (P, S, D), F32, kind="Internal").ap()

        s_x0T_in = sem("x0T_in")
        s_gate_in = sem("gate_in")
        s_xtok_in = sem("xtok_in")
        s_bias_in = sem("bias_in")
        s_wo_in = sem("wo_in")
        s_small_in = sem("small_in")
        s_s3_in = sem("s3_in")
        s_const_ok = sem("const_ok")
        s_wp_hi_ok = sem("wp_hi_ok")
        s_wp_lo_ok = sem("wp_lo_ok")
        s_wo_hi_ok = sem("wo_hi_ok")
        s_wo_lo_ok = sem("wo_lo_ok")
        s_xs_hi_ok = sem("xs_hi_ok")
        s_xs_lo_ok = sem("xs_lo_ok")
        s_q_mm = sem("q_mm")
        s_k_mm = sem("k_mm")
        s_a_mm = sem("a_mm")
        s_v_mm = sem("v_mm")
        s_q_out = sem("q_out")
        s_k_out = sem("k_out")
        s_al_out = sem("al_out")
        s_v_out = sem("v_out")
        s_abs_ok = sem("abs_ok")
        s_exp_ok = sem("exp_ok")
        s_ln_ok = sem("ln_ok")
        s_qk_ok = sem("qk_ok")
        s_sgn_ok = sem("sgn_ok")
        s_sp_sum = sem("sp_sum")
        s_sp_ok = sem("sp_ok")
        s_b_red = sem("b_red")
        s_gate_again = sem("gate_again")
        s_ba_T = sem("ba_T")
        s_chain = sem("chain")
        s_tab_d = sem("tab_d")
        s_tab_exp = sem("tab_exp")
        s_A_ok = sem("A_ok")
        s_B_T = sem("B_T")
        s_BtokOK = sem("BtokOK")
        s_A_out = sem("A_out")
        s_vsize_ok = sem("vsize_ok")
        s_extremes_ok = sem("extremes_ok")
        s_extremes_T = sem("extremes_T")
        s_flag_ok = sem("flag_ok")
        s_attn_ready = sem("attn_ready")
        s_fall_v = sem("fall_v")
        s_fall_vin = sem("fall_vin")
        s_fall_step = sem("fall_step")
        s_fall_chain = sem("fall_chain")
        s_fall_r = sem("fall_r")
        s_fall_rin = sem("fall_rin")
        s_fall_sum = sem("fall_sum")
        s_scan_ok = sem("scan_ok")
        s_start_ok = sem("start_ok")
        s_spread = sem("spread")
        s_M_ok = sem("M_ok")
        s_Mhi_ok = sem("Mhi_ok")
        s_vhi_ok = sem("vhi_ok")
        s_Mlo_ok = sem("Mlo_ok")
        s_vlo_ok = sem("vlo_ok")
        s_y_mm = sem("y_mm")
        s_yhi_ok = sem("yhi_ok")
        s_ylo_ok = sem("ylo_ok")
        s_o_mm = sem("o_mm")
        s_res_ok = sem("res_ok")
        s_bn_tick = sem("bn_tick")
        s_bn_ok = sem("bn_ok")
        s_mv_ok = sem("mv_ok")
        s_ve_ok = sem("ve_ok")
        s_rstd_ok = sem("rstd_ok")
        s_xn_ok = sem("xn_ok")
        s_xkeep_ok = sem("xkeep_ok")
        s_xT_mm = sem("xT_mm")
        s_xThi_ok = sem("xThi_ok")
        s_xTlo_ok = sem("xTlo_ok")
        s_up_mm = sem("up_mm")
        s_relu_ok = sem("relu_ok")
        s_hlo_ok = sem("hlo_ok")
        s_down_mm = sem("down_mm")
        s_gated_ok = sem("gated_ok")
        s_wxhi_ok = sem("wxhi_ok")
        s_wxlo_ok = sem("wxlo_ok")
        s_stage_used = sem("stage_used")
        s_st_cmp = sem("st_cmp")
        s_wide_c = sem("wide_c")
        s_wide_a = sem("wide_a")
        s_wide_f = sem("wide_f")
        s_raw_in = sem("raw_in")
        s_f_bn = sem("f_bn")
        s_f_mv = sem("f_mv")
        s_f_ve = sem("f_ve")
        s_f_rstd = sem("f_rstd")
        s_f_xn = sem("f_xn")
        s_f_keep = sem("f_keep")
        s_f_T = sem("f_T")
        s_f_xhi = sem("f_xhi")
        s_f_xlo = sem("f_xlo")
        s_f_first = sem("f_first")
        s_f_mm = sem("f_mm")
        s_l_out = sem("l_out")
        s_f_silu = sem("f_silu")
        s_f_hf = sem("f_hf")
        s_f_hi = sem("f_hi")
        s_f_lo = sem("f_lo")
        s_e_y = sem("e_y")
        s_e_mul = sem("e_mul")
        s_e_add = sem("e_add")
        s_e_bn = sem("e_bn")
        s_e_mv = sem("e_mv")
        s_e_ve = sem("e_ve")
        s_e_rstd = sem("e_rstd")
        s_e_xo = sem("e_xo")
        wp_in = [sem(f"wp_in{n}") for n in range(4)]
        abc_in = [sem(f"abc_in{j}") for j in range(J)]
        stage_in = [sem(f"stage_in{u}") for u in range(2)]
        wx_in = [[sem(f"wx_in{e}"), sem(f"wx_out{e}")] for e in range(2)]
        out_done = [sem(f"out_done{j}") for j in range(J)]

        block = stack.enter_context(nc.Block())

        def groups(eng, body, *more):
            with eng.Fori(0, G - 1) as g:
                body(g, False, *more)
            body(G - 1, True, *more)

        def groups_behind(eng, body):
            body(0, True, False)
            with eng.Fori(1, G - 1) as g:
                body(g, False, False)
            body(G - 1, False, True)

        def steps(eng, step, *more):
            step(-1, False, True, True, *more)
            with eng.Fori(0, G - 2) as g:
                step(g, True, True, True, *more)
            step(G - 2, True, True, False, *more)
            step(G - 1, True, False, False, *more)

        def pairs_of_experts(eng, body):
            with eng.Fori(1, E // 2 - 1) as p:
                body(p, False)
            body(E // 2 - 1, True)

        SPREAD = [bank[4:6], bank[6:8], bank[0:2], bank[2:4]]
        IN, OUT = slice(0, DC * DX), slice(DC * DX, WX)

        COLS = {"q": (0, HD), "k": (HD, HD), "a": (2 * HD, HD), "v": (3 * HD, D)}

        def step_path_dma(sp_):
            sp_.dma_start(v_dram.rearrange("b t d -> t b d"), v_sb[:, :, :]).then_inc(s_fall_v, 16)
            sp_.wait_ge(s_fall_v, 16)
            with sp_.Fori(0, S) as t:
                sp_.wait_ge(s_fall_step, t + 1)
                sp_.dma_start(v_now[:, :], v_dram[:, bass.ds(t, 1), :].rearrange("b o d -> b (o d)").unsqueeze(1).to_broadcast([B, H, D])
                              ).then_inc(s_fall_vin, 16)
                sp_.wait_ge(s_fall_r, t + 1)
                sp_.dma_start(r_dram[:, bass.ds(t, 1), :].rearrange("p o d -> p (o d)"), r_now[:, :]).then_inc(s_fall_rin, 16)
            sp_.wait_ge(s_fall_rin, 16 * S + 16)
            with sp_.Fori(0, B) as b:
                sp_.wait_ge(s_fall_sum, b + 1)
                sp_.dma_start(r_heads[:, :, :], r_dram[bass.ds(b * H, H)].rearrange("h t d -> t h d")).then_inc(s_fall_rin, 16)
            sp_.wait_ge(s_fall_sum, B + 1)
            sp_.dma_start(a_dram, AT[:, :]).then_inc(s_A_out, 16)
            sp_.wait_ge(s_A_out, 32)

        def step_path(dve):
            dve.wait_ge(s_start_ok, J)
            dve.wait_ge(s_spread, J)
            dve.sem_inc(s_fall_step, 1)
            dve.sem_inc(s_fall_rin, 16)
            dve.sem_inc(s_fall_sum, 1)
            dve.memset(r_now[:, :], 0.0)
            with dve.Fori(0, S) as t:
                a_t, b_t = AT[:, bass.ds(t, 1)], BT[:, bass.ds(t, 1)]
                dve.wait_ge(s_fall_vin, t * 16 + 16)
                dve.tensor_scalar(n_now[:, :], v_now[:, :], b_t, None, ALU.mult).then_inc(s_fall_step, 1)
                dve.wait_ge(s_fall_step, t + 2)
                dve.scalar_tensor_tensor(out=raw_now[:, :], in0=r_now[:, :], scalar=a_t, in1=n_now[:, :],
                                         op0=ALU.mult, op1=ALU.add)
                dve.scalar_tensor_tensor(out=mx_now[:, :], in0=r_now[:, :], scalar=a_t, in1=n_now[:, :],
                                         op0=ALU.mult, op1=ALU.max)
                dve.scalar_tensor_tensor(out=sg_now[:, :], in0=r_now[:, :], scalar=a_t, in1=n_now[:, :],
                                         op0=ALU.mult, op1=ALU.min).then_inc(s_fall_chain, 1)
                dve.wait_ge(s_fall_chain, t * 4 + 1)
                dve.scalar_tensor_tensor(out=mx_now[:, :], in0=sg_now[:, :], scalar=-1.0, in1=mx_now[:, :],
                                         op0=ALU.mult, op1=ALU.max).then_inc(s_fall_chain, 1)
                dve.wait_ge(s_fall_chain, t * 4 + 2)
                dve.tensor_scalar(sg_now[:, :], raw_now[:, :], 0.0, 2.0, ALU.is_ge, ALU.mult).then_inc(s_fall_chain, 1)
                dve.wait_ge(s_fall_chain, t * 4 + 3)
                dve.scalar_tensor_tensor(out=sg_now[:, :], in0=sg_now[:, :], scalar=1.0, in1=mx_now[:, :],
                                         op0=ALU.subtract, op1=ALU.mult).then_inc(s_fall_chain, 1)
                dve.wait_ge(s_fall_chain, t * 4 + 4)
                dve.wait_ge(s_fall_rin, t * 16 + 16)
                dve.scalar_tensor_tensor(out=r_now[:, :], in0=sg_now[:, :], scalar=EPS, in1=raw_now[:, :],
                                         op0=ALU.mult, op1=ALU.add).then_inc(s_fall_r, 1)
                dve.wait_ge(s_fall_r, t + 1)
            dve.memset(AT[:, :], 0.0)
            dve.memset(B_tok[:, :], 1.0 / H)
            for j in range(J):
                for i in range(2):
                    dve.memset(SPREAD[j][i][:, :], 0.0)
            with dve.Fori(0, B) as b:
                dve.wait_ge(s_fall_rin, 16 * S + 16 + 16 + b * 16)
                dve.tensor_reduce(v_sb[:, bass.ds(b, 1)].rearrange("p o d -> p (o d)"), r_heads[:, :, :].rearrange("p h d -> p d h"),
                                  AX_X, ALU.add).then_inc(s_fall_sum, 1)
            dve.wait_ge(s_fall_sum, B + 1)
            for n in range(J * H):
                diagonal = dve.tensor_scalar(decay[:, n // H, n % H * S:n % H * S + S], ident[:, :], 1.0 / H, None, ALU.mult)
            diagonal.then_inc(s_fall_sum, 1)
            dve.wait_ge(s_fall_sum, B + 2)

        @block.sync
        def _(sp_):
            for i, name in enumerate("aqkv"):
                c0, n = COLS[name]
                sp_.dma_start(wp_raw[:, :, c0:c0 + n], wproj[:, :, c0:c0 + n]).then_inc(wp_in[i], 16)
                if i == 0:
                    sp_.dma_start(x0T[:, 0:J], xT[:, 0:J]).then_inc(s_x0T_in, 16)
                if i == 0:
                    sp_.dma_start(bias_b[:, :], alpha_b.partition_broadcast(P)).then_inc(s_bias_in, 16)
            for g in range(G):
                a, b = slice(J * g, J * g + J), slice(J * g + J, J * g + 2 * J)
                if g > 0:
                    sp_.wait_ge(s_gate_in, 32 * g)
                sp_.dma_start(ctx_sb[:, a], ctx[:, a]).then_inc(s_gate_in, 16)
                sp_.dma_start(itok_sb[:, a], itok[:, a]).then_inc(s_gate_in, 16)
                if g < G - 1:
                    sp_.wait_ge(s_x0T_in, 16 * g + 16)
                    sp_.dma_start(x0T[:, b], xT[:, b]).then_inc(s_x0T_in, 16)
            sp_.dma_start(wo_raw[:, :, :], wo).then_inc(s_wo_in, 16)
            sp_.dma_start(x_tok[:, :, :], x.rearrange("b t d -> t b d")).then_inc(s_xtok_in, 16)
            sp_.dma_start(scales[:, :, :], ffn_s).then_inc(s_small_in, 16)
            for e in range(2):
                for i, part in enumerate((IN, OUT)):
                    sp_.dma_start(wx_raw[:, e, part], wx[e, :, part]).then_inc(wx_in[e][i], 16)

            sp_.wait_ge(s_A_ok, 1)
            sp_.dma_start(a_dram, AT[:, :]).then_inc(s_A_out, 16)
            sp_.wait_ge(s_flag_ok, 1)
            stepwise = sp_.value_load(flag[0:1, 0:1], min_val=0, max_val=1)
            sp_.wait_ge(s_A_out, 16)
            with sp_.If(stepwise > 0):
                step_path_dma(sp_)
            with sp_.Else():
                sp_.nop()

            def decays(g):
                for j in range(J):
                    sp_.wait_ge(s_scan_ok, g * J + j + 1)
                    sp_.dma_start(a_bc[:, j], a_dram[bass.ds((g * J + j) * H, H), :].rearrange("h s -> (h s)").partition_broadcast(P)
                                  ).then_inc(abc_in[j], 16)
            with sp_.Fori(1, G) as g:
                decays(g)

            def load_expert(e, expert, units):
                sp_.wait_ge(s_up_mm, units * XC)
                sp_.dma_start(wx_raw[:, e, IN], wx[bass.ds(expert, 1), :, IN].rearrange("e p w -> p (e w)")).then_inc(wx_in[e][0], 16)
                sp_.wait_ge(s_down_mm, (units + 2) * J)
                sp_.dma_start(wx_raw[:, e, OUT], wx[bass.ds(expert, 1), :, OUT].rearrange("e p w -> p (e w)")).then_inc(wx_in[e][1], 16)
            sp_.wait_ge(s_M_ok, B + J)
            sp_.dma_start(ctx_sb[:, :, :], ctx).then_inc(s_gate_again, 16)
            sp_.dma_start(itok_sb[:, :, :], itok).then_inc(s_gate_again, 16)
            load_expert(0, 2, 7)

            def pair(p, last):
                for u in range(8):
                    if not last or u < 6:
                        for i in range(2):
                            n = ((p - 1) * 8 + u) * 2 + i
                            sp_.wait_ge(s_stage_used, n + 1)
                            sp_.dma_start(stage[:, i], wffn[:, bass.ds(n * PIECE, PIECE)]).then_inc(stage_in[i], 16)
                    if u == 0:
                        load_expert(1, p * 2 + 1, p * 8)
                    if u == 4 and not last:
                        load_expert(0, p * 2 + 2, p * 8 + 4)
            pairs_of_experts(sp_, pair)
            sp_.wait_ge(s_up_mm, E * G * XC)
            sp_.dma_start(s3_b[:, :], w3_s.partition_broadcast(P)).then_inc(s_s3_in, 16)
            sp_.wait_ge(s_wide_f, 1)
            wide = sp_.value_load(wide_flag[0:1, 0:1], min_val=0, max_val=1)

            with sp_.If(wide > 0):
                sp_.dma_start(wf_raw[:, :], wffn).then_inc(s_raw_in, 16)
            with sp_.Else():
                sp_.nop()

            with sp_.Fori(0, G) as g:
                for j in range(J):
                    sp_.wait_ge(s_e_xo, g * J + j + 1)
                    sp_.dma_start(out[bass.ds(g * J + j, 1)].rearrange("b t d -> t (b d)"), xo[:, j]).then_inc(out_done[j], 16)
            for j in range(J):
                sp_.wait_ge(out_done[j], 16 * G + 16)

        @block.gpsimd
        def _(pool):
            pool.memset(ident[:, :], 0.0).then_inc(s_const_ok, 1)
            pool.memset(neghalf[:, :], -0.5)
            for e in range(E):
                pool.memset(expert_no[:, e:e + 1], float(e))
            pool.wait_ge(s_const_ok, 1)
            pool.affine_select(out=ident[:, :], in_=ident[:, :], compare_op=ALU.not_equal, fill=1.0, base=0,
                               pattern=[[-1, P]], channel_multiplier=1).then_inc(s_const_ok, 1)
            pool.wait_ge(s_const_ok, 2)

            def low_half(t, j):
                pool.wait_ge(s_xs_hi_ok, t + 1)
                pool.tensor_tensor(xs_lo[:, j], x0T[:, bass.ds(t, 1)].rearrange("p o c s -> p (o c) s"), xs_hi[:, j].bitcast(F32),
                                   ALU.subtract).then_inc(s_xs_lo_ok, 1)

            for j in range(J):
                low_half(j, j)

            def project(g, last):
                for j in range(J):
                    t = g * J + j
                    pool.wait_ge(s_k_out, t + 3)
                    pool.wait_ge(s_b_red, t + 1)
                    pool.tensor_tensor(qk[:, j % 2], q_sb[:, j % 2], k_sb[:, j % 2], ALU.mult).then_inc(s_qk_ok, 1)
                    if not last:
                        pool.wait_ge(s_v_mm, t + 1)
                        low_half(t + J, j)
            groups(pool, project)

            def expert_low(e, n):
                for c in range(4):
                    pool.wait_ge(s_wxhi_ok, n * 4 + c + 1)
                    a = slice(c * WX // 4, (c + 1) * WX // 4)
                    pool.tensor_tensor(wx_lo[:, e, a], wx_raw[:, e, a], wx_hi[:, e, a].bitcast(F32), ALU.subtract).then_inc(s_wxlo_ok, 1)
            expert_low(0, 0)

            def start(g, j):
                pool.wait_ge(s_M_ok, g * J + j + 1)
                pool.tensor_tensor(decay[:, j].rearrange("p (h s) -> p h s", h=H), ident[:, :].unsqueeze(1).to_broadcast([P, H, S]),
                                   B_tok[:, bass.ds((g * J + j) * H, H)].unsqueeze(2).to_broadcast([P, H, S]),
                                   ALU.mult).then_inc(s_start_ok, 1)

            def halves_v(g):
                for j in range(J):
                    pool.wait_ge(s_vhi_ok, g * J + j + 1)
                    pool.tensor_tensor(vs_lo[:, j], v_sb[:, bass.ds(g * J + j, 1)].rearrange("p o d -> p (o d)"), vs_hi[:, j].bitcast(F32),
                                       ALU.subtract).then_inc(s_vlo_ok, 1)

            def halves_M(g):
                for j in range(J):
                    pool.wait_ge(s_Mhi_ok, g * J + j + 1)
                    pool.tensor_tensor(M_lo[:, j], M_f[:, j], M_hi[:, j].bitcast(F32), ALU.subtract).then_inc(s_Mlo_ok, 1)

            def root(g):
                pool.wait_ge(s_ve_ok, g + 1)
                pool.tensor_tensor(rstd[:, :], var_eps[:, :], neghalf[:, :], ALU.pow).then_inc(s_rstd_ok, 1)

            def step(g, units, back, front):
                if front:
                    for j in range(J):
                        start(g + 2, j)
                if back:
                    root(g + 1)
                if front:
                    halves_v(g + 2)
                if not units:
                    expert_low(1, 1)
                if front:
                    halves_M(g + 2)
            pool.wait_ge(s_BtokOK, 1)
            for j in range(J):
                start(0, j)
            pool.wait_ge(s_attn_ready, 1)
            halves_v(0)
            halves_M(0)
            steps(pool, step)

            expert_low(0, 2)

            def pair(p, last):
                expert_low(1, p * 2 + 1)
                if not last:
                    expert_low(0, p * 2 + 2)
            pairs_of_experts(pool, pair)

            def ln_rstd(sem_in, sem_out, n):
                pool.wait_ge(sem_in, n)
                pool.tensor_tensor(rstd[:, :], var_eps[:, :], neghalf[:, :], ALU.pow).then_inc(sem_out, 1)
            ln_rstd(s_f_ve, s_f_rstd, 1)
            pool.wait_ge(s_wide_c, 1)
            pool.partition_all_reduce(wide_all[:, :], wide_col[:, :], P, RMAX).then_inc(s_wide_a, 1)
            pool.wait_ge(s_wide_f, 1)
            wide = pool.value_load(wide_flag[0:1, 0:1], min_val=0, max_val=1)

            def ffn(g, last, exact):
                if exact:
                    for n in range(3 * FC):
                        pool.wait_ge(s_f_hi, g * 3 * FC + n + 1)
                        dst, hi = [(ha_lo, ha_hi), (hb_lo, hb_hi), (ha_lo, ha_hi)][n // FC]
                        pool.tensor_tensor(dst[:, n % FC], hf[:, n % 3], hi[:, n % FC].bitcast(F32), ALU.subtract).then_inc(s_f_lo, 1)
                        if n == FC + 2 and not last:
                            ln_rstd(s_f_ve, s_f_rstd, g + 2)
                elif not last:
                    ln_rstd(s_f_ve, s_f_rstd, g + 2)
                ln_rstd(s_e_ve, s_e_rstd, g + 1)

            with pool.If(wide > 0):
                groups(pool, ffn, False)
                pool.nop()
            with pool.Else():
                groups(pool, ffn, True)
                pool.nop()

        @block.scalar
        def _(act):
            act.preload_act_table_set("natural_log_exp_and_others")
            act.sem_inc(s_q_out, 2)
            act.sem_inc(s_k_out, 2)
            act.sem_inc(s_vsize_ok, 2)

            def high_half(t, j):
                act.activation(xs_hi[:, j], x0T[:, bass.ds(t, 1)].rearrange("p o c s -> p (o c) s"), ACT.Copy).then_inc(s_xs_hi_ok, 1)

            def size_v(t, r):
                act.wait_ge(s_v_out, t + 3)
                act.wait_ge(s_vsize_ok, t + 1)
                act.activation(v_size[:, r], v_sb[:, bass.ds(t, 1)].rearrange("p o d -> p (o d)"), ACT.Abs,
                               accum_out=v_sizes[:, bass.ds(t, 1)]).then_inc(s_vsize_ok, 1)

            for n, name in enumerate("aqkv"):
                c0, cn = COLS[name]
                act.wait_ge(wp_in[n], 16)
                act.activation(wp_hi[:, :, c0:c0 + cn], wp_raw[:, :, c0:c0 + cn], ACT.Copy).then_inc(s_wp_hi_ok, 1)
                if n == 0:
                    act.wait_ge(s_x0T_in, 16)
                    for j in range(J):
                        high_half(j, j)

            def project(g, first, last):
                for j in range(J):
                    t, r = g * J + j, j % 2
                    act.wait_ge(s_al_out, t + 3)
                    act.wait_ge(s_sp_ok, t + 1)
                    act.activation(sp[:, r], al[:, r], ACT.Abs).then_inc(s_abs_ok, 1)
                    act.wait_ge(s_abs_ok, t + 1)
                    act.activation(sp[:, r], sp[:, r], ACT.Exp, scale=-1.0).then_inc(s_exp_ok, 1)
                    act.wait_ge(s_q_mm, t + 1)
                    act.wait_ge(s_qk_ok, t + 1)
                    act.activation(q_sb[:, r], bank[r * 3 + 1][:, :], ACT.Copy).then_inc(s_q_out, 1)
                    act.wait_ge(s_exp_ok, t + 1)
                    act.activation(sp[:, r], sp[:, r], ACT.Ln, bias=1.0).then_inc(s_ln_ok, 1)
                    act.wait_ge(s_k_mm, t + 1)
                    act.activation(k_sb[:, r], bank[r * 3 + 2][:, :], ACT.Copy).then_inc(s_k_out, 1)
                    if not last:
                        act.wait_ge(s_v_mm, t + 1)
                        act.wait_ge(s_x0T_in, 16 * g + 32)
                        high_half(t + J, j)
                    if j > 0 or not first:
                        size_v(t - 1, 1 - r)
            groups_behind(act, project)
            size_v(B - 1, 1)

            def expert_high(e, n):
                for c in range(4):
                    if c % 2 == 0:
                        act.wait_ge(wx_in[e][c // 2], (n - e) * 8 + 16)
                    a = slice(c * WX // 4, (c + 1) * WX // 4)
                    act.activation(wx_hi[:, e, a], wx_raw[:, e, a], ACT.Copy).then_inc(s_wxhi_ok, 1)
            act.wait_ge(s_wo_in, 16)
            act.activation(wo_hi[:, :, :], wo_raw[:, :, :], ACT.Copy).then_inc(s_wo_hi_ok, 1)
            expert_high(0, 0)

            act.wait_ge(s_tab_d, 2)
            act.activation(decT[:, :], decT[:, :], ACT.Exp).then_inc(s_tab_exp, 1)
            act.activation(betT[:, :], betT[:, :], ACT.Exp).then_inc(s_tab_exp, 1)
            expert_high(1, 1)

            act.wait_ge(s_attn_ready, 1)

            def halves_v(g):
                for j in range(J):
                    act.wait_ge(s_y_mm, g * J + j + 1)
                    act.activation(vs_hi[:, j], v_sb[:, bass.ds(g * J + j, 1)].rearrange("p o d -> p (o d)"), ACT.Copy).then_inc(s_vhi_ok, 1)

            def half_M(g, j):
                act.wait_ge(s_M_ok, g * J + j + 1 + J)
                act.activation(M_hi[:, j], M_f[:, j], ACT.Copy).then_inc(s_Mhi_ok, 1)

            def halves_y(g):
                for j in range(J):
                    act.wait_ge(s_y_mm, g * J + j + 1 + J)
                    act.wait_ge(s_o_mm, g * J + j + 1)
                    act.activation(yT_hi[:, j], bank[4 + j][:, 0:D].rearrange("p (c s) -> p c s", c=DC), ACT.Copy).then_inc(s_yhi_ok, 1)

            def keep_x(g):
                for j in range(J):
                    act.wait_ge(s_xn_ok, g * J + j + 1)
                    act.activation(x_tok[:, bass.ds(g * J + j, 1)].rearrange("p o d -> p (o d)"), xn[:, j], ACT.Copy).then_inc(s_xkeep_ok, 1)

            def halves_x(g):
                for j in range(J):
                    act.wait_ge(s_xT_mm, g * J + j + 1)
                    act.activation(xT_hi[:, :, bass.ds((g * J + j) * S, S)], bank[4 + j][:, 0:D].rearrange("p (c s) -> p c s", c=DC),
                                   ACT.Copy).then_inc(s_xThi_ok, 1)

            def relu(unit, place, c, b):
                act.wait_ge(s_up_mm, unit * XC + c + 1)
                act.wait_ge(s_down_mm, (unit + 1) * J)
                act.activation(hx_hi[:, place, c], bank[b][:, :], ACT.Relu).then_inc(s_relu_ok, 1)

            def step(g, units, back, front):
                for c in range(XC):
                    if units:
                        relu(g * 2, 0, c, c % 2)
                    if c == 1 and back:
                        halves_y(g + 1)
                if front:
                    halves_v(g + 2)
                for c in range(XC):
                    if units:
                        relu(g * 2 + 1, 1, c, c % 2)
                    if c == 2 and back:
                        keep_x(g + 1)
                    if c == XC - 1 and front and units:
                        half_M(g + 2, 0)
                if back:
                    halves_x(g + 1)
                if front:
                    for j in range(1 if units else 0, J):
                        half_M(g + 2, j)
            halves_v(0)
            for j in range(J):
                half_M(0, j)
            steps(act, step)
            expert_high(0, 2)

            def keep(n0):
                for j in range(J):
                    act.wait_ge(s_f_xn, n0 + j + 1)
                    act.activation(x_tok[:, bass.ds(n0 + j, 1)].rearrange("p o d -> p (o d)"), xn2[:, j], ACT.Copy).then_inc(s_f_keep, 1)

            def norm2_T(n0, exact, done=s_f_xhi):
                for j in range(J):
                    act.wait_ge(s_f_T, n0 + j + 1)
                    src = bank[4 + j][:, 0:D].rearrange("p (c s) -> p c s", c=DC)
                    dst = (xf_hi if exact else xf_wide)[:, :, j * S:j * S + S]
                    act.activation(dst, src, ACT.Copy).then_inc(done, 1)

            def pair(p, last):
                for u in range(8):
                    for c in range(XC):
                        relu(p * 8 + u, u % 2, c, 4 + c if u == 0 else c % 2)
                    if u == 1:
                        expert_high(1, p * 2 + 1)
                    if u == 5 and not last:
                        expert_high(0, p * 2 + 2)
                    if u == 7 and last:
                        keep(0)
                        norm2_T(0, True)
            pairs_of_experts(act, pair)

            act.wait_ge(s_wide_f, 1)
            wide = act.value_load(wide_flag[0:1, 0:1], min_val=0, max_val=1)

            def ffn(g, last, exact):
                for n in range(3 * FC):
                    layer, m = divmod(n, FC)
                    act.wait_ge(s_f_mm, (g * 3 * FC + n) + 1)
                    if layer == 0:
                        act.wait_ge(s_f_hf, g * FC + m + 3)
                        act.activation(silu[:, m % 2], bank[2 * (m % 4)][:, :], ACT.Silu, scale=scales[:, 0, m:m + 1]).then_inc(s_f_silu, 1)
                    else:
                        b = bank[m % 4]
                        if exact:
                            act.wait_ge(s_f_lo, g * 3 * FC + n + 1)
                            act.activation(hf[:, n % 3], b[:, :], ACT.Gelu, scale=scales[:, 1 + layer, m:m + 1]).then_inc(s_l_out, 1)
                        else:
                            dst = [hb_wide, ha_wide][layer - 1]
                            act.activation(dst[:, m], b[:, :], ACT.Gelu, scale=scales[:, 1 + layer, m:m + 1]).then_inc(s_l_out, 1)
                    if n == 2 * FC - 1 and not last:
                        keep((g + 1) * J)
                        norm2_T((g + 1) * J, exact)

            with act.If(wide > 0):
                act.wait_ge(s_f_xlo, J)
                norm2_T(0, False, s_f_first)
                groups(act, ffn, False)
                act.nop()
            with act.Else():
                groups(act, ffn, True)
                act.nop()

        @block.tensor
        def _(pe):

            def product(dst, pairs, inc=None):
                for n, (a, b) in enumerate(pairs):
                    mm = pe.matmul(dst, a, b, start=(n == 0), stop=(n == len(pairs) - 1))
                if inc is not None:
                    mm.then_inc(inc, 1)
                return mm

            def three(a_hi, a_lo, b_hi, b_lo):
                return [(a_hi, b_hi), (a_hi, b_lo), (a_lo, b_hi)]

            def project(g, last):
                for j in range(J):
                    t, r = g * J + j, j % 2
                    pe.wait_ge(s_xs_lo_ok, t + 1)
                    for n, name in enumerate("aqkv"):
                        c0, cn = COLS[name]
                        pe.wait_ge(s_wp_lo_ok, n + 1)
                        pe.wait_ge((s_al_out, s_q_out, s_k_out, s_v_out)[n], t + 1)
                        dst = bank[6 + r][:, 0:D] if name == "v" else bank[r * 3 + n][:, :]
                        product(dst, [pair for c in range(DC) for pair in three(
                            xs_hi[:, j, c], xs_lo[:, j, c], wp_hi[:, c, c0:c0 + cn], wp_lo[:, c, c0:c0 + cn])],
                            (s_a_mm, s_q_mm, s_k_mm, s_v_mm)[n])
            pe.wait_ge(s_const_ok, 2)
            groups(pe, project)

            pe.wait_ge(s_sp_ok, B + 2)
            pe.wait_ge(s_b_red, B + 2)
            pe.wait_ge(s_q_out, B + 2)
            pe.wait_ge(s_k_out, B + 2)
            pe.transpose(bank[0][:, 0:P], b_tok[:, :, :].rearrange("p b h -> p (b h)"), ident[:, :]).then_inc(s_ba_T, 1)
            pe.transpose(bank[1][:, 0:P], a_tok[:, :, :].rearrange("p b h -> p (b h)"), ident[:, :]).then_inc(s_ba_T, 1)
            pe.wait_ge(s_chain, 8)
            pe.transpose(bank[2][:, 0:P], BT[:, :], ident[:, :]).then_inc(s_B_T, 1)
            pe.wait_ge(s_extremes_ok, 1)
            for i in range(3):
                mm = pe.transpose(bank[3][0:1, i * P:i * P + P], extremes[:, i:i + 1], ident[:, :])
            mm.then_inc(s_extremes_T, 1)
            pe.wait_ge(s_A_ok, 1)
            pe.wait_ge(s_v_out, B + 2)
            pe.wait_ge(s_al_out, B + 2)
            for j in range(J):
                if j == J - 1:
                    pe.wait_ge(s_flag_ok, 1)
                for h in range(H):
                    n = j * H + h
                    mm = pe.matmul(SPREAD[j][h // 4][:, h % 4 * S:h % 4 * S + S], ident[:, n:n + 1].to_broadcast([P, P]), AT[:, :],
                                   start=True, stop=True)
                mm.then_inc(s_spread, 1)
            pe.wait_ge(s_attn_ready, 1)
            pe.wait_ge(s_wo_lo_ok, 1)

            def mixed(g):
                for j in range(J):
                    t = g * J + j
                    pe.wait_ge(s_Mlo_ok, t + 1)
                    pe.wait_ge(s_vlo_ok, t + 1)
                    pe.wait_ge(s_xTlo_ok, t + 1)
                    for c in range(DC):
                        a = slice(c * P, c * P + P)
                        mm = product(bank[4 + j][:, a], three(vs_hi[:, j, a], vs_lo[:, j, a], M_hi[:, j], M_lo[:, j]))
                    mm.then_inc(s_y_mm, 1)

            def projected(g):
                for j in range(J):
                    t = g * J + j
                    pe.wait_ge(s_ylo_ok, t + 1)
                    pe.wait_ge(s_res_ok, t + 1)
                    product(bank[4 + j][:, D:2 * D], [pair for c in range(DC) for pair in three(
                        yT_hi[:, j, c], yT_lo[:, j, c], wo_hi[:, c], wo_lo[:, c])], s_o_mm)

            def turned(g):
                for j in range(J):
                    pe.wait_ge(s_xn_ok, g * J + j + 1)
                    pe.transpose(bank[4 + j][:, 0:P], xn[:, j, 0:P], ident[:, :])
                    pe.transpose(bank[4 + j][:, P:2 * P], xn[:, j, P:2 * P], ident[:, :]).then_inc(s_xT_mm, 1)

            def up(unit, e, g, c, expert, b):
                if c == 0:
                    pe.wait_ge(s_xTlo_ok, g * J + 2 * J)
                    pe.wait_ge(s_wxlo_ok, expert * 4 + 2)
                wi_hi = wx_hi[:, e, IN].rearrange("p (c d) -> p c d", c=DC)
                wi_lo = wx_lo[:, e, IN].rearrange("p (c d) -> p c d", c=DC)
                if b < 2:
                    pe.wait_ge(s_hlo_ok, unit * XC + c + 1)
                a, cols = slice(c * P, c * P + P), bass.ds(g * N, N)
                product(bank[b][:, :], [pair for i in range(DC) for pair in three(
                    wi_hi[:, i, a], wi_lo[:, i, a], xT_hi[:, i, cols], xT_lo[:, i, cols])], s_up_mm)

            def down(unit, place, e, j, expert):
                wo_h = wx_hi[:, e, OUT].rearrange("p (c d) -> p c d", c=XC)
                wo_l = wx_lo[:, e, OUT].rearrange("p (c d) -> p c d", c=XC)
                if j == 0:
                    pe.wait_ge(s_wxlo_ok, expert * 4 + 4)
                pe.wait_ge(s_gated_ok, unit * J + j + 1)
                a = slice(j * S, j * S + S)
                for c in range(XC):
                    if j == 0:
                        pe.wait_ge(s_hlo_ok, unit * XC + c + 1 + 2)
                    for i, (x_, w_) in enumerate(three(hx_hi[:, place, c, a], hx_lo[:, place, c, a], wo_h[:, c], wo_l[:, c])):
                        mm = pe.matmul(bank[2 + j % 2][:, 0:D], x_, w_, start=(c == 0 and i == 0), stop=(c == XC - 1 and i == 2))
                mm.then_inc(s_down_mm, 1)

            def step(g, units, back, front):
                for c in range(XC):
                    if units:
                        up(g * 2, 0, g, c, 0, c % 2)
                    if c == 1 and back:
                        mixed(g + 1)
                if back:
                    projected(g + 1)
                if units:
                    for c in range(XC):
                        up(g * 2 + 1, 1, g, c, 1, c % 2)
                        down(g * 2, 0, 0, c, 0)
                if back:
                    turned(g + 1)
                if units:
                    for j in range(J):
                        down(g * 2 + 1, 1, 1, j, 1)

            pe.sem_inc(s_y_mm, J)
            pe.sem_inc(s_o_mm, J)
            pe.sem_inc(s_down_mm, 2 * J)
            steps(pe, step)

            def norm2_T(n0):
                for j in range(J):
                    pe.wait_ge(s_f_xn, n0 + j + 1)
                    pe.transpose(bank[4 + j][:, 0:P], xn2[:, j, 0:P], ident[:, :])
                    pe.transpose(bank[4 + j][:, P:2 * P], xn2[:, j, P:2 * P], ident[:, :]).then_inc(s_f_T, 1)

            def pair(p, last):
                for c in range(XC):
                    up(p * 8, 0, 0, c, p * 2, 4 + c)
                for u in range(8):
                    for c in range(XC):
                        if u == 7 and last and c == 2:
                            norm2_T(0)
                        if u < 7:
                            up(p * 8 + u + 1, (u + 1) // G, (u + 1) % G, c, p * 2 + (u + 1) // G, c % 2)
                        down(p * 8 + u, u % 2, u // G, c, p * 2 + u // G)
            pairs_of_experts(pe, pair)

            pe.wait_ge(s_wide_f, 1)
            wide = pe.value_load(wide_flag[0:1, 0:1], min_val=0, max_val=1)

            W1, W2, H1, H2, W3 = 0, DC * F, 2 * DC * F, 2 * DC * F + FC * F, 2 * DC * F + 2 * FC * F

            def ffn(g, last, exact):
                wf = wf_hi if exact else wf_raw
                x_parts = [xf_hi, xf_lo] if exact else [xf_wide]
                a_parts = [ha_hi, ha_lo] if exact else [ha_wide]
                b_parts = [hb_hi, hb_lo] if exact else [hb_wide]
                pe.wait_ge(s_f_xlo if exact else s_f_xhi, g * J + J)
                for m in range(FC):
                    r = 2 * (m % 4)
                    if m == 1:
                        pe.wait_ge(s_gated_ok, B * E + 2)
                    if m == 2:
                        pe.wait_ge(s_e_mul, g * J + 1)
                    for o, b in ((W1, r), (W2, r + 1)):
                        pe.wait_ge(s_f_hf, g * FC + m + 1)
                        mm = product(bank[b][:, :], [(wf[:, o + c * F + m * P:o + c * F + m * P + P], part[:, c])
                                                     for c in range(DC) for part in x_parts])
                    mm.then_inc(s_f_mm, 1)
                for layer, (o, parts) in enumerate(((H1, a_parts), (H2, b_parts))):
                    for m in range(FC):
                        n = (layer + 1) * FC + m
                        if m < 4:
                            pe.wait_ge(s_f_hf, g * FC + FC - 2 + 4) if layer == 0 else pe.wait_ge(s_l_out, (g * 2 + layer) * FC - 4 + m + 1)
                        else:
                            pe.wait_ge(s_l_out, (g * 2 + layer) * FC + m - 4 + 1)
                        for k in range(FC):
                            if m == 0:
                                if exact:
                                    pe.wait_ge(s_f_lo, g * 3 * FC + layer * FC + k + 4)
                                elif layer == 0:
                                    pe.wait_ge(s_f_hf, g * FC + k + 1 + 4)
                                else:
                                    pe.wait_ge(s_l_out, g * 2 * FC + k + 1)
                            for i, part in enumerate(parts):
                                mm = pe.matmul(bank[m % 4][:, :], wf[:, o + k * F + m * P:o + k * F + m * P + P], part[:, k],
                                               start=(k == 0 and i == 0), stop=(k == FC - 1 and i == len(parts) - 1))
                        mm.then_inc(s_f_mm, 1)
                    if layer == 0 and not last:
                        norm2_T((g + 1) * J)
                if not last:
                    pe.wait_ge(s_f_xlo if exact else s_f_xhi, (g + 2) * J)
                for pair in ((0, 1), (2, 3)):
                    for k in range(FC):
                        if pair[0] == 0:
                            pe.wait_ge(s_f_lo, g * 3 * FC + 2 * FC + k + 4) if exact else pe.wait_ge(s_l_out, g * 2 * FC + FC + k + 1)
                        for j in pair:
                            a = slice(j * S, j * S + S)
                            for i, part in enumerate(a_parts):
                                mm = pe.matmul(bank[4 + j][:, 0:D], part[:, k, a], wf[:, W3 + k * D:W3 + k * D + D],
                                               start=(k == 0 and i == 0), stop=(k == FC - 1 and i == len(a_parts) - 1))
                            if k == FC - 1:
                                mm.then_inc(s_e_y, 1)

            with pe.If(wide > 0):
                pe.wait_ge(s_raw_in, 16)
                pe.wait_ge(s_f_first, J)
                groups(pe, ffn, False)
                pe.nop()
            with pe.Else():
                groups(pe, ffn, True)
                pe.nop()

        @block.vector
        def _(dve):
            dve.sem_inc(s_al_out, 2)
            dve.sem_inc(s_v_out, 2)
            dve.sem_inc(s_b_red, 2)
            dve.sem_inc(s_qk_ok, 2)
            dve.sem_inc(s_sp_ok, 2)
            dve.sem_inc(s_scan_ok, J)
            dve.sem_inc(s_M_ok, J)
            for n, name in enumerate("aqkv"):
                c0, cn = COLS[name]
                dve.wait_ge(s_wp_hi_ok, n + 1)
                dve.tensor_tensor(wp_lo[:, :, c0:c0 + cn], wp_raw[:, :, c0:c0 + cn], wp_hi[:, :, c0:c0 + cn].bitcast(F32),
                                  ALU.subtract).then_inc(s_wp_lo_ok, 1)
            dve.wait_ge(s_bias_in, 16)
            dve.wait_ge(s_const_ok, 2)

            def gate(b, e, scratch):
                dve.scalar_tensor_tensor(
                    out=scratch, in0=itok_sb[:, bass.ds(b, 1)].rearrange("p b k -> p (b k)"), scalar=expert_no[:, bass.ds(e, 1)],
                    in1=ctx_sb[:, bass.ds(b, 1)].rearrange("p b k -> p (b k)"), op0=ALU.is_equal, op1=ALU.mult,
                    accum_out=gates[:, bass.ds(b, 1), bass.ds(e, 1)].rearrange("p b e -> p (b e)"))

            def end_tile(t, r):
                dve.wait_ge(s_v_mm, t + 1)
                dve.tensor_scalar(sgn[:, :], bank[6 + r][:, 0:D], 0.0, 2 * EPS, ALU.is_ge, ALU.mult).then_inc(s_sgn_ok, 1)
                dve.wait_ge(s_sgn_ok, t + 1)
                dve.scalar_tensor_tensor(out=v_sb[:, bass.ds(t, 1)].rearrange("p o d -> p (o d)"), in0=sgn[:, :], scalar=EPS,
                                         in1=bank[6 + r][:, 0:D], op0=ALU.subtract, op1=ALU.add).then_inc(s_v_out, 1)
                dve.wait_ge(s_qk_ok, t + 3)
                dve.tensor_reduce(b_tok[:, bass.ds(t, 1)].rearrange("p o h -> p (o h)"), qk[:, r].rearrange("p (h d) -> p h d", h=H),
                                  AX_X, ALU.add).then_inc(s_b_red, 1)

            def project(g, first, last):
                for j in range(J):
                    t, r = g * J + j, j % 2
                    dve.wait_ge(s_gate_in, 32 * g + 32)
                    dve.wait_ge(s_a_mm, t + 1)
                    dve.tensor_tensor(al[:, r], bank[r * 3][:, :], bias_b[:, :], ALU.add).then_inc(s_al_out, 1)
                    if j > 0 or not first:
                        end_tile(t - 1, 1 - r)
                    if j < J - 1 or not last:
                        for e in range(4):
                            gate(t, e, masked[:, e])
                    dve.wait_ge(s_ln_ok, t + 1)
                    dve.scalar_tensor_tensor(out=sp[:, r], in0=al[:, r], scalar=0.0, in1=sp[:, r], op0=ALU.max,
                                             op1=ALU.add).then_inc(s_sp_sum, 1)
                    dve.wait_ge(s_sp_sum, t + 1)
                    dve.tensor_reduce(a_tok[:, bass.ds(t, 1)].rearrange("p o h -> p (o h)"), sp[:, r].rearrange("p (h d) -> p h d", h=H),
                                      AX_X, ALU.add).then_inc(s_sp_ok, 1)
            groups_behind(dve, project)
            end_tile(B - 1, 1)
            for e in range(4):
                gate(B - 1, e, masked[:, e])

            chain = [0]

            def link(instruction):
                instruction.then_inc(s_chain, 1)
                chain[0] += 1
                dve.wait_ge(s_chain, chain[0])

            dve.wait_ge(s_ba_T, 2)
            dve.tensor_scalar(bT[:, :], bank[0][:, 0:S], SCALE, None, ALU.mult)
            link(dve.tensor_scalar(aT[:, :], bank[1][:, 0:S], -1.0, None, ALU.mult))
            link(dve.memset(aT[:, 0:1], 0.0))
            link(dve.tensor_tensor_scan(mT[:, :], aT[:, :], bT[:, :], LOWEST, ALU.add, ALU.max))
            dve.tensor_tensor(betT[:, :], bT[:, :], mT[:, :], ALU.subtract).then_inc(s_tab_d, 1)
            link(dve.tensor_tensor(decT[:, 1:S], aT[:, 1:S], mT[:, 0:S - 1], ALU.add))
            dve.memset(decT[:, 0:1], 0.0)
            dve.tensor_tensor(decT[:, 1:S], decT[:, 1:S], mT[:, 1:S], ALU.subtract).then_inc(s_tab_d, 1)
            dve.wait_ge(s_vsize_ok, B + 2)
            dve.tensor_reduce(extremes[:, 1:2], v_sizes[:, :], AX_X, ALU.max)
            dve.wait_ge(s_wo_hi_ok, 1)
            dve.tensor_tensor(wo_lo[:, :, :], wo_raw[:, :, :], wo_hi[:, :, :].bitcast(F32), ALU.subtract).then_inc(s_wo_lo_ok, 1)
            dve.wait_ge(s_tab_exp, 2)
            link(dve.memset(decT[:, 0:1], 0.0))
            link(dve.tensor_tensor_scan(eT[:, :], decT[:, :], betT[:, :], 0.0, ALU.mult, ALU.add))
            link(dve.reciprocal(rT[:, :], eT[:, :]))
            link(dve.tensor_tensor(BT[:, :], betT[:, :], rT[:, :], ALU.mult))
            dve.memset(AT[:, 0:1], 0.0)
            link(dve.tensor_tensor(AT[:, 1:S], decT[:, 1:S], eT[:, 0:S - 1], ALU.mult))
            dve.tensor_tensor(AT[:, :], AT[:, :], rT[:, :], ALU.mult).then_inc(s_A_ok, 1)
            dve.tensor_reduce(extremes[:, 2:3], BT[:, :], AX_X, ALU.min)
            dve.wait_ge(s_A_ok, 1)
            dve.tensor_reduce(extremes[:, 0:1], AT[:, :], AX_X, ALU.max).then_inc(s_extremes_ok, 1)
            dve.wait_ge(s_B_T, 1)
            dve.tensor_copy(B_tok[:, :], bank[2][:, 0:S]).then_inc(s_BtokOK, 1)
            dve.wait_ge(s_extremes_T, 1)
            rows = bank[3][0:1, 0:3 * P].rearrange("o (i n) -> o i n", i=3)
            dve.tensor_reduce(extreme[0:1, 0:2], rows[:, 0:2], AX_X, ALU.max)
            link(dve.tensor_reduce(extreme[0:1, 2:3], rows[:, 2], AX_X, ALU.min))
            dve.tensor_scalar(products[0:1, 0:1], extreme[0:1, 0:1], extreme[0:1, 1:2], None, ALU.mult)
            link(dve.tensor_scalar(products[0:1, 1:2], extreme[0:1, 2:3], EPS / 2.02, None, ALU.mult))
            dve.tensor_tensor(flag[0:1, :], products[0:1, 0:1], products[0:1, 1:2], ALU.is_gt).then_inc(s_flag_ok, 1)
            dve.wait_ge(s_flag_ok, 1)
            dve.wait_ge(s_BtokOK, 1)
            stepwise = dve.value_load(flag[0:1, 0:1], min_val=0, max_val=1)
            with dve.If(stepwise > 0):
                step_path(dve)
                dve.nop()
            with dve.Else():
                dve.nop()
            dve.sem_inc(s_res_ok, J)
            dve.sem_inc(s_xTlo_ok, J)
            dve.sem_inc(s_hlo_ok, 2)
            dve.sem_inc(s_gated_ok, 2)
            dve.sem_inc(s_stage_used, 2)
            dve.sem_inc(s_f_hf, 4)
            dve.sem_inc(s_f_lo, 3)
            dve.sem_inc(s_e_mul, 1)
            dve.wait_ge(s_xtok_in, 16)
            dve.sem_inc(s_attn_ready, 1)

            def norm_means(n0, stats, means, var):
                for j in range(J):
                    dve.wait_ge(stats, n0 + j + 1)
                    dve.sem_inc(s_bn_tick, 1)
                    dve.bn_aggr(mv[:, j], bn[:, j]).then_inc(means, 1)
                dve.wait_ge(means, n0 + J)
                dve.tensor_scalar(var_eps[:, :], mv[:, :, 1], LN_EPS, None, ALU.add).then_inc(var, 1)

            def norm_apply(row, dst, g, root, normed):
                dve.wait_ge(root, g + 1)
                for j in range(J):
                    dve.tensor_scalar(dst[:, j], row(j), mv[:, j, 0:1], rstd[:, j:j + 1], ALU.subtract, ALU.mult).then_inc(normed, 1)

            def scan(g, j):
                dve.wait_ge(abc_in[j], 16 * g)
                dve.wait_ge(s_start_ok, g * J + j + 1)
                dve.tensor_tensor_scan(decay[:, j], a_bc[:, j], decay[:, j], 0.0, ALU.mult, ALU.add).then_inc(s_scan_ok, 1)

            def sum_heads(g, j):
                dve.wait_ge(s_scan_ok, g * J + j + 1 + J)
                dve.tensor_reduce(M_f[:, j], decay[:, j].rearrange("p (h s) -> p s h", h=H), AX_X, ALU.add).then_inc(s_M_ok, 1)

            def halves_y(g):
                for j in range(J):
                    dve.wait_ge(s_yhi_ok, g * J + j + 1)
                    dve.tensor_tensor(yT_lo[:, j], bank[4 + j][:, 0:D].rearrange("p (c s) -> p c s", c=DC), yT_hi[:, j].bitcast(F32),
                                      ALU.subtract).then_inc(s_ylo_ok, 1)

            def group_row(g, j):
                return x_tok[:, bass.ds(g * J + j, 1)].rearrange("p o d -> p (o d)")

            def residual(g):
                for j in range(J):
                    dve.wait_ge(s_o_mm, g * J + j + 1 + J)
                    dve.tensor_tensor(group_row(g, j), bank[4 + j][:, D:2 * D], group_row(g, j), ALU.add).then_inc(s_res_ok, 1)
                    dve.wait_ge(s_res_ok, g * J + j + 1 + J)
                    dve.sem_inc(s_bn_tick, 1)
                    dve.bn_stats(bn[:, j], group_row(g, j)).then_inc(s_bn_ok, 1)
                norm_means(g * J, s_bn_ok, s_mv_ok, s_ve_ok)

            def halves_x(g):
                for j in range(J):
                    dve.wait_ge(s_xThi_ok, g * J + j + 1)
                    cols = bass.ds((g * J + j) * S, S)
                    dve.tensor_tensor(xT_lo[:, :, cols], bank[4 + j][:, 0:D].rearrange("p (c s) -> p c s", c=DC),
                                      xT_hi[:, :, cols].bitcast(F32), ALU.subtract).then_inc(s_xTlo_ok, 1)

            def low(unit, place, c, b):
                dve.wait_ge(s_relu_ok, unit * XC + c + 1)
                dve.scalar_tensor_tensor(out=hx_lo[:, place, c], in0=bank[b][:, :], scalar=0.0, in1=hx_hi[:, place, c].bitcast(F32),
                                         op0=ALU.max, op1=ALU.subtract).then_inc(s_hlo_ok, 1)

            def gated(unit, g, j, expert):
                dve.wait_ge(s_down_mm, unit * J + j + 1 + 2 * J)
                dve.wait_ge(s_gated_ok, unit * J + j + 1)
                gate = gates[:, bass.ds(g * J + j, 1), bass.ds(expert, 1)].rearrange("p b e -> p (b e)")
                dve.scalar_tensor_tensor(out=group_row(g, j), in0=bank[2 + j % 2][:, 0:D], scalar=gate, in1=group_row(g, j),
                                         op0=ALU.mult, op1=ALU.add).then_inc(s_gated_ok, 1)

            def step(g, units, back, front):
                for c in range(XC):
                    if units:
                        low(g * 2, 0, c, c % 2)
                    if c == (1 if units else 0) and back:
                        halves_y(g + 1)
                    if c in (1, 2) and front:
                        scan(g + 2, c - 1)
                if back:
                    residual(g + 1)
                if front:
                    scan(g + 2, 2)
                if units:
                    low(g * 2 + 1, 1, 0, 0)
                for c in range(XC):
                    if units:
                        if c < XC - 1:
                            low(g * 2 + 1, 1, c + 1, (c + 1) % 2)
                        gated(g * 2, g, c, 0)
                    if c == 0 and back:
                        norm_apply(lambda j: group_row(g + 1, j), xn, g + 1, s_rstd_ok, s_xn_ok)
                    if front:
                        if c == 0:
                            scan(g + 2, 3)
                        elif c == 1 and units:
                            sum_heads(g + 2, 0)
                for j in range(J):
                    if units:
                        gated(g * 2 + 1, g, j, 1)
                    if j == 0 and back:
                        halves_x(g + 1)
                    if front and not (units and j == 0):
                        sum_heads(g + 2, j)

            for j in range(J):
                dve.wait_ge(s_spread, j + 1)
                dve.wait_ge(s_start_ok, j + 1)
                for i in range(2):
                    half = slice(i * H // 2 * S, (i + 1) * H // 2 * S)
                    scanned = dve.tensor_tensor_scan(decay[:, j, half], SPREAD[j][i][:, :], decay[:, j, half], 0.0, ALU.mult, ALU.add)
                scanned.then_inc(s_scan_ok, 1)
                if j > 0:
                    sum_heads(0, j - 1)
            sum_heads(0, J - 1)
            steps(dve, step)

            def take_piece(p, u, i):
                n = ((p - 1) * 8 + u) * 2 + i
                dve.wait_ge(stage_in[i], (n - i) * 8 + 16)
                dve.tensor_copy(wf_hi[:, bass.ds(n * PIECE, PIECE)], stage[:, i]).then_inc(s_st_cmp, 1)
                dve.wait_ge(s_st_cmp, n + 1)
                dve.scalar_tensor_tensor(out=stage[:, i], in0=stage[:, i], scalar=1.0, in1=wf_hi[:, bass.ds(n * PIECE, PIECE)].bitcast(F32),
                                         op0=ALU.mult, op1=ALU.not_equal, accum_out=neq[:, bass.ds(n, 1)]).then_inc(s_stage_used, 1)

            def norm2_stats(n0):
                for j in range(J):
                    dve.bn_stats(bn[:, j], x_tok[:, bass.ds(n0 + j, 1)].rearrange("p o d -> p (o d)")).then_inc(s_f_bn, 1)
                norm_means(n0, s_f_bn, s_f_mv, s_f_ve)

            def norm2_apply(n0, g):
                norm_apply(lambda j: x_tok[:, bass.ds(n0 + j, 1)].rearrange("p o d -> p (o d)"), xn2, g, s_f_rstd, s_f_xn)

            def norm2_low(n0):
                for j in range(J):
                    dve.wait_ge(s_f_xhi, n0 + j + 1)
                    src = bank[4 + j][:, 0:D].rearrange("p (c s) -> p c s", c=DC)
                    cols = slice(j * S, j * S + S)
                    dve.tensor_tensor(xf_lo[:, :, cols], src, xf_hi[:, :, cols].bitcast(F32), ALU.subtract).then_inc(s_f_xlo, 1)

            def pair(p, last):
                for c in range(XC):
                    low(p * 8, 0, c, 4 + c)
                for u in range(8):
                    for c in range(XC):
                        if u < 7:
                            low(p * 8 + u + 1, (u + 1) % 2, c, c % 2)
                        if u == 7 and c == 3 and last:
                            norm2_low(0)
                        gated(p * 8 + u, u % G, c, p * 2 + u // G)
                        if c < 2 and (not last or u < 6):
                            take_piece(p, u, c)
                        if not last:
                            gate(u * 2 + c // 2, p * 2 + 2 + c % 2, masked_late[:, c])
                    if u == 5 and last:
                        dve.wait_ge(s_stage_used, PIECES + 2)
                        dve.tensor_reduce(wide_col[:, :], neq[:, :], AX_X, ALU.max).then_inc(s_wide_c, 1)
                        norm2_stats(0)
                    if u == 6 and last:
                        norm2_apply(0, 0)
                        dve.wait_ge(s_wide_a, 1)
                        dve.tensor_scalar(wide_flag[:, :], wide_all[:, :], 0.0, None, ALU.is_gt).then_inc(s_wide_f, 1)
            dve.wait_ge(s_gate_again, 32)
            pairs_of_experts(dve, pair)

            dve.wait_ge(s_gated_ok, B * E + 2)
            dve.wait_ge(s_wide_f, 1)
            wide = dve.value_load(wide_flag[0:1, 0:1], min_val=0, max_val=1)
            dve.wait_ge(s_s3_in, 16)
            dve.wait_ge(s_small_in, 16)

            def ffn(g, last, exact):
                for n in range(3 * FC):
                    layer, m = divmod(n, FC)
                    dst = [ha_hi, hb_hi, ha_hi][layer]
                    if layer == 0:
                        dve.wait_ge(s_f_silu, g * FC + m + 1)
                        if exact:
                            dve.wait_ge(s_f_lo, g * 3 * FC + n + 1)
                            o = hf[:, n % 3]
                        else:
                            o = ha_wide[:, m]
                        dve.scalar_tensor_tensor(out=o, in0=bank[2 * (m % 4) + 1][:, :], scalar=scales[:, 1, m:m + 1], in1=silu[:, m % 2],
                                                 op0=ALU.mult, op1=ALU.mult).then_inc(s_f_hf, 1)
                        if exact:
                            dve.wait_ge(s_f_hf, g * FC + m + 1 + 4)
                    elif exact:
                        dve.wait_ge(s_l_out, g * 2 * FC + (layer - 1) * FC + m + 1)
                    if exact:
                        dve.tensor_copy(dst[:, m], hf[:, n % 3]).then_inc(s_f_hi, 1)
                    if n == FC + 2 and not last:
                        norm2_stats((g + 1) * J)
                        norm2_apply((g + 1) * J, g + 1)
                    if n == 2 * FC + 1 and not last and exact:
                        norm2_low((g + 1) * J)
                for j in range(J):
                    t = g * J + j
                    dve.wait_ge(s_e_y, t + 1)
                    dve.tensor_tensor(y_s[:, j % 2], bank[4 + j][:, 0:D], s3_b[:, :], ALU.mult).then_inc(s_e_mul, 1)
                    dve.wait_ge(s_e_mul, t + 2)
                    row = x_tok[:, bass.ds(t, 1)].rearrange("p o d -> p (o d)")
                    dve.tensor_tensor(row, y_s[:, j % 2], row, ALU.add).then_inc(s_e_add, 1)
                    dve.wait_ge(s_e_add, t + 1)
                    dve.sem_inc(s_bn_tick, 1)
                    dve.bn_stats(bn[:, j], row).then_inc(s_e_bn, 1)
                for j in range(J):
                    dve.wait_ge(out_done[j], 16 * g + 16)
                norm_means(g * J, s_e_bn, s_e_mv, s_e_ve)
                norm_apply(lambda j: group_row(g, j), xo, g, s_e_rstd, s_e_xo)

            for j in range(J):
                dve.sem_inc(out_done[j], 16)
            with dve.If(wide > 0):
                groups(dve, ffn, False)
                dve.nop()
            with dve.Else():
                groups(dve, ffn, True)
                dve.nop()


def tiled(w, chunks):
    return np.ascontiguousarray(np.asarray(w).T.reshape(chunks, P, -1).transpose(1, 0, 2))


def laid_out(i):
    a = {k: np.asarray(v) for k, v in i.items()}
    words = lambda *ws: np.ascontiguousarray(np.concatenate([w.reshape(P, -1) for w in ws], axis=1))
    return {
        "x": np.ascontiguousarray(a["x"]),
        "xT": np.ascontiguousarray(a["x"].reshape(B, S, DC, P).transpose(3, 0, 2, 1)),
        "wproj": np.concatenate([tiled(a["L0_attn_" + n], DC) for n in ("W_q", "W_k", "W_alpha_w", "W_v")], axis=2),
        "wo": tiled(a["L0_attn_W_o"], DC),
        "alpha_b": np.ascontiguousarray(a["L0_attn_W_alpha_b"]),
        "ctx": np.ascontiguousarray(a["ctx_512"].transpose(2, 0, 1)),
        "itok": np.ascontiguousarray(a["itok_BxS2xS_0_7"].transpose(2, 0, 1)),
        "wx": np.stack([words(tiled(a["L0_xattn_proj_in"][e], DC), tiled(a["L0_xattn_proj_out"][e], XC)) for e in range(E)]),
        "wffn": words(tiled(a["L0_ffn_w1_w"], DC), tiled(a["L0_ffn_w2_w"], DC), tiled(a["L0_ffn_h1_w"], FC),
                      tiled(a["L0_ffn_h2_w"], FC), tiled(a["L0_ffn_w3_w"], FC)),
        "ffn_s": np.ascontiguousarray(np.stack([a["L0_ffn_" + n].reshape(FC, P).T for n in ("w1_s", "w2_s", "h1_s", "h2_s")], axis=1)),
        "w3_s": np.ascontiguousarray(a["L0_ffn_w3_s"]),
    }


def kernel(**inputs):
    import concourse.bacc as bacc
    from concourse.bass_utils import run_bass_kernel_spmd

    nc = bacc.Bacc("TRN2", target_bir_lowering=False, num_devices=1)
    arrays, args = {}, []
    for name, array in laid_out(inputs).items():
        arrays[f"in_{name}"] = array
        args.append(nc.dram_tensor(f"in_{name}", array.shape, mybir.dt.from_np(array.dtype), kind="ExternalInput").ap())
    args.append(nc.dram_tensor("out_0", (B, S, D), F32, kind="ExternalOutput").ap())
    decoder_kernel(nc, *args)
    return run_bass_kernel_spmd(nc, [arrays], core_ids=[0]).results[0]["out_0"]
```
